# Optimizing a Trainium2 kernel written in Bass

```python
import numpy as np
import jax
import jax.numpy as jnp

def _softmax(x, axis=-1):
    return jax.nn.softmax(x, axis=axis)
def _gelu(x):
    return jax.nn.gelu(x, approximate=True)
def _silu(x):
    return jax.nn.silu(x)
def _sigmoid(x):
    return jax.nn.sigmoid(x)
def _layernorm(x, axis=-1, eps=1e-5):
    m = jnp.mean(x, axis=axis, keepdims=True)
    v = jnp.var(x, axis=axis, keepdims=True)
    return (x - m) / jnp.sqrt(v + eps)
def _scatter_add(tgt, idx, src, axis=0):
    return tgt.at[idx].add(src)
def _segment_sum(src, seg, n):
    return jax.ops.segment_sum(src, seg, n)

kernel_name = 'mk_adj_preln_d4_adj_128_44762a'

def setup_inputs(seed: int = 0):
    np.random.seed(seed)
    _w = jnp.asarray
    def _rec_inputs():
        import jax
        import jax.numpy as jnp
        _gk = jax.random.key(seed)
        x = -0.001547 + 1.001 * jax.random.normal(jax.random.fold_in(_gk, 1), (128, 64, 128), jnp.float32)
        _a = jax.random.bernoulli(jax.random.fold_in(_gk, 2), 0.125, (128, 64, 64))
        _a = jnp.logical_or(_a, jnp.swapaxes(_a, -1, -2))
        _a = jnp.logical_or(_a, jnp.eye(64, dtype=bool))
        _af = _a.astype(jnp.float32)
        _af = _af * jax.random.uniform(jax.random.fold_in(_gk, 3), (128, 64, 64), jnp.float32, 0.05, 4.99997)
        adj = _af
        return x, adj
    x, adj = _rec_inputs()
    def _L0_gnn_setup():
        import jax, jax.numpy as jnp
        import numpy as np
        B, N, NAB, NF, NG = (8, 256, 128, 128, 64)
        CUTOFF = 5.0
        LN2 = float(np.log(2.0))

        def ssp(x):
            return jax.nn.softplus(x) - LN2
        key = jax.random.key(seed)
        ks = jax.random.split(key, 12)
        r = jax.random.normal(ks[0], (B, N, NAB), dtype=jnp.float32)
        e = jax.random.uniform(ks[1], (B, N, N), dtype=jnp.float32) * CUTOFF
        A = (jax.random.uniform(ks[2], (B, N, N)) < 0.3).astype(jnp.float32)
        s = 0.05
        W1 = jax.random.normal(ks[3], (NF, NG), dtype=jnp.float32) * s
        b1 = jnp.zeros((NF,), jnp.float32)
        W2 = jax.random.normal(ks[4], (NF, NF), dtype=jnp.float32) * s
        b2 = jnp.zeros((NF,), jnp.float32)
        Wa = jax.random.normal(ks[5], (NF, NAB), dtype=jnp.float32) * s
        Wd1 = jax.random.normal(ks[6], (NAB, NF), dtype=jnp.float32) * s
        bd1 = jnp.zeros((NAB,), jnp.float32)
        Wd2 = jax.random.normal(ks[7], (NAB, NAB), dtype=jnp.float32) * s
        bd2 = jnp.zeros((NAB,), jnp.float32)
        return {'r': r, 'e': e, 'A': A, 'W1': W1, 'b1': b1, 'W2': W2, 'b2': b2, 'Wa': Wa, 'Wd1': Wd1, 'bd1': bd1, 'Wd2': Wd2, 'bd2': bd2}
    _L0_gnn_all = _L0_gnn_setup()
    _L0_gnn_in = {k: v for k, v in _L0_gnn_all.items() if k in ('W1', 'b1', 'W2', 'b2', 'Wa', 'Wd1', 'bd1', 'Wd2', 'bd2', )}
    del _L0_gnn_all

    def _L1_gnn_setup():
        import jax, jax.numpy as jnp
        import numpy as np
        MIN_NORM = 1e-15
        PROJ_EPS = 0.004
        C = 1.0

        def artanh(x):
            return jnp.arctanh(jnp.clip(x, -1.0 + 1e-07, 1.0 - 1e-07))

        def _norm(x):
            return jnp.clip(jnp.linalg.norm(x, axis=-1, keepdims=True), MIN_NORM, None)

        def proj(x, c):
            n = _norm(x)
            maxnorm = (1.0 - PROJ_EPS) / jnp.sqrt(c)
            return jnp.where(n > maxnorm, x / n * maxnorm, x)

        def expmap0(u, c):
            sc = jnp.sqrt(c)
            un = _norm(u)
            return jnp.tanh(sc * un) * u / (sc * un)

        def logmap0(p, c):
            sc = jnp.sqrt(c)
            pn = _norm(p)
            return artanh(sc * pn) * p / (sc * pn)

        def mobius_add(x, y, c):
            x2 = jnp.sum(x * x, -1, keepdims=True)
            y2 = jnp.sum(y * y, -1, keepdims=True)
            xy = jnp.sum(x * y, -1, keepdims=True)
            num = (1.0 + 2.0 * c * xy + c * y2) * x + (1.0 - c * x2) * y
            den = 1.0 + 2.0 * c * xy + c * c * x2 * y2
            return num / jnp.clip(den, MIN_NORM, None)

        def lambda_x(x, c):
            x2 = jnp.sum(x * x, -1, keepdims=True)
            return 2.0 / jnp.clip(1.0 - c * x2, MIN_NORM, None)

        def expmap(u, p, c):
            sc = jnp.sqrt(c)
            un = _norm(u)
            second = jnp.tanh(0.5 * sc * lambda_x(p, c) * un) * u / (sc * un)
            return mobius_add(p, second, c)

        def logmap(p1, p2, c):
            sub = mobius_add(-p1, p2, c)
            sn = _norm(sub)
            sc = jnp.sqrt(c)
            return 2.0 / (sc * lambda_x(p1, c)) * artanh(sc * sn) * sub / sn

        def mobius_matvec(m, x, c):
            sc = jnp.sqrt(c)
            xn = _norm(x)
            mx = x @ m.T
            mxn = _norm(mx)
            res = jnp.tanh(mxn / xn * artanh(sc * xn)) * mx / (mxn * sc)
            zero_row = jnp.all(mx == 0, axis=-1, keepdims=True)
            return jnp.where(zero_row, jnp.zeros_like(res), res)
        key = jax.random.key(seed)
        ks = jax.random.split(key, 12)
        b, n, d = (4, 256, 128)
        x = 0.01 * jax.random.normal(ks[0], (b, n, d), dtype=jnp.float32)
        mask = (jax.random.uniform(ks[1], (b, n, n)) < 0.15).astype(jnp.float32)
        s = 0.05
        return {'x': x, 'mask': mask, 'W': s * jax.random.normal(ks[2], (d, d), dtype=jnp.float32), 'b_lin': jnp.zeros((d,), dtype=jnp.float32), 'att_w1': s * jax.random.normal(ks[3], (d, 2 * d), dtype=jnp.float32), 'att_b1': jnp.zeros((d,), dtype=jnp.float32), 'att_w2': s * jax.random.normal(ks[4], (1, d), dtype=jnp.float32), 'att_b2': jnp.zeros((1,), dtype=jnp.float32), 'mlp_w1': s * jax.random.normal(ks[5], (d, 2 * d), dtype=jnp.float32), 'mlp_b1': jnp.zeros((d,), dtype=jnp.float32), 'mlp_w2': s * jax.random.normal(ks[6], (d, d), dtype=jnp.float32), 'mlp_b2': jnp.zeros((d,), dtype=jnp.float32)}
    _L1_gnn_all = _L1_gnn_setup()
    _L1_gnn_in = {k: v for k, v in _L1_gnn_all.items() if k in ('W', 'b_lin', 'att_w1', 'att_b1', 'att_w2', 'att_b2', 'mlp_w1', 'mlp_b1', 'mlp_w2', 'mlp_b2', )}
    del _L1_gnn_all

    def _L2_gnn_setup():
        import jax, jax.numpy as jnp
        import numpy as np
        B, N, DIN, DOUT = (8, 2048, 128, 128)
        key = jax.random.key(seed)
        k1, k2, k3, k4 = jax.random.split(key, 4)
        x = jax.random.normal(k1, (B, N, DIN), dtype=jnp.float32)
        adj = jax.random.uniform(k2, (B, N, N), dtype=jnp.float32)
        W = jax.random.normal(k3, (DIN, DOUT), dtype=jnp.float32) / np.sqrt(DIN)
        b = jax.random.normal(k4, (DOUT,), dtype=jnp.float32) * 0.01
        return {'x': x, 'adj': adj, 'W': W, 'b': b}
    _L2_gnn_all = _L2_gnn_setup()
    _L2_gnn_in = {k: v for k, v in _L2_gnn_all.items() if k in ('W', 'b', )}
    del _L2_gnn_all

    def _L3_gnn_setup():
        import jax, jax.numpy as jnp
        import numpy as np
        UNITS = 128
        D_FEAT = 128
        B, N = (4, 4096)
        EDGE_PROB = 0.01
        key = jax.random.key(seed)
        k1, k2, k3, k4 = jax.random.split(key, 4)
        x = jax.random.normal(k1, (B, N, D_FEAT), dtype=jnp.float32)
        adj = (jax.random.uniform(k2, (B, N, N)) < EDGE_PROB).astype(jnp.float32)
        W_msg = jax.random.normal(k3, (2 * D_FEAT, UNITS), dtype=jnp.float32) / np.sqrt(2 * D_FEAT).astype(np.float32)
        W_upd = jax.random.normal(k4, (D_FEAT + UNITS, UNITS), dtype=jnp.float32) / np.sqrt(D_FEAT + UNITS).astype(np.float32)
        return {'x': x, 'adj': adj, 'W_msg': W_msg, 'W_upd': W_upd}
    _L3_gnn_all = _L3_gnn_setup()
    _L3_gnn_in = {k: v for k, v in _L3_gnn_all.items() if k in ('W_msg', 'W_upd', )}
    del _L3_gnn_all

    return {
        "x": x,
        "adj": adj,
        "L0_gnn_W1": _L0_gnn_in["W1"],
        "L0_gnn_b1": _L0_gnn_in["b1"],
        "L0_gnn_W2": _L0_gnn_in["W2"],
        "L0_gnn_b2": _L0_gnn_in["b2"],
        "L0_gnn_Wa": _L0_gnn_in["Wa"],
        "L0_gnn_Wd1": _L0_gnn_in["Wd1"],
        "L0_gnn_bd1": _L0_gnn_in["bd1"],
        "L0_gnn_Wd2": _L0_gnn_in["Wd2"],
        "L0_gnn_bd2": _L0_gnn_in["bd2"],
        "L1_gnn_W": _L1_gnn_in["W"],
        "L1_gnn_b_lin": _L1_gnn_in["b_lin"],
        "L1_gnn_att_w1": _L1_gnn_in["att_w1"],
        "L1_gnn_att_b1": _L1_gnn_in["att_b1"],
        "L1_gnn_att_w2": _L1_gnn_in["att_w2"],
        "L1_gnn_att_b2": _L1_gnn_in["att_b2"],
        "L1_gnn_mlp_w1": _L1_gnn_in["mlp_w1"],
        "L1_gnn_mlp_b1": _L1_gnn_in["mlp_b1"],
        "L1_gnn_mlp_w2": _L1_gnn_in["mlp_w2"],
        "L1_gnn_mlp_b2": _L1_gnn_in["mlp_b2"],
        "L2_gnn_W": _L2_gnn_in["W"],
        "L2_gnn_b": _L2_gnn_in["b"],
        "L3_gnn_W_msg": _L3_gnn_in["W_msg"],
        "L3_gnn_W_upd": _L3_gnn_in["W_upd"],
    }

def reference(x, adj, L0_gnn_W1, L0_gnn_b1, L0_gnn_W2, L0_gnn_b2, L0_gnn_Wa, L0_gnn_Wd1, L0_gnn_bd1, L0_gnn_Wd2, L0_gnn_bd2, L1_gnn_W, L1_gnn_b_lin, L1_gnn_att_w1, L1_gnn_att_b1, L1_gnn_att_w2, L1_gnn_att_b2, L1_gnn_mlp_w1, L1_gnn_mlp_b1, L1_gnn_mlp_w2, L1_gnn_mlp_b2, L2_gnn_W, L2_gnn_b, L3_gnn_W_msg, L3_gnn_W_upd):
    import jax
    import jax.numpy as jnp
    def _L0_gnn_ref(r, e, A, W1, b1, W2, b2, Wa, Wd1, bd1, Wd2, bd2):
        import jax, jax.numpy as jnp
        import numpy as np
        B, N, NAB, NF, NG = (8, 256, 128, 128, 64)
        CUTOFF = 5.0
        LN2 = float(np.log(2.0))

        def ssp(x):
            return jax.nn.softplus(x) - LN2
        offsets = jnp.linspace(0.0, CUTOFF, NG, dtype=jnp.float32)
        width = offsets[1] - offsets[0]
        coeff = -0.5 / (width * width)
        diff = e[:, :, :, None] - offsets
        g = jnp.exp(coeff * diff * diff)
        h = ssp(jnp.einsum('bijg,fg->bijf', g, W1) + b1)
        Wf = jnp.einsum('bijf,gf->bijg', h, W2) + b2
        rf = jnp.einsum('bjd,fd->bjf', r, Wa)
        Am = A[:, :, :, None]
        Wf = Wf * Am
        y = jnp.einsum('bjf,bijf->bif', rf, Wf * Am)
        y = ssp(jnp.einsum('bif,df->bid', y, Wd1) + bd1)
        y = jnp.einsum('bid,ed->bie', y, Wd2) + bd2
        return y

    def _L1_gnn_ref(x, mask, W, b_lin, att_w1, att_b1, att_w2, att_b2, mlp_w1, mlp_b1, mlp_w2, mlp_b2):
        import jax, jax.numpy as jnp
        import numpy as np
        MIN_NORM = 1e-15
        PROJ_EPS = 0.004
        C = 1.0

        def artanh(x):
            return jnp.arctanh(jnp.clip(x, -1.0 + 1e-07, 1.0 - 1e-07))

        def _norm(x):
            return jnp.clip(jnp.linalg.norm(x, axis=-1, keepdims=True), MIN_NORM, None)

        def proj(x, c):
            n = _norm(x)
            maxnorm = (1.0 - PROJ_EPS) / jnp.sqrt(c)
            return jnp.where(n > maxnorm, x / n * maxnorm, x)

        def expmap0(u, c):
            sc = jnp.sqrt(c)
            un = _norm(u)
            return jnp.tanh(sc * un) * u / (sc * un)

        def logmap0(p, c):
            sc = jnp.sqrt(c)
            pn = _norm(p)
            return artanh(sc * pn) * p / (sc * pn)

        def mobius_add(x, y, c):
            x2 = jnp.sum(x * x, -1, keepdims=True)
            y2 = jnp.sum(y * y, -1, keepdims=True)
            xy = jnp.sum(x * y, -1, keepdims=True)
            num = (1.0 + 2.0 * c * xy + c * y2) * x + (1.0 - c * x2) * y
            den = 1.0 + 2.0 * c * xy + c * c * x2 * y2
            return num / jnp.clip(den, MIN_NORM, None)

        def lambda_x(x, c):
            x2 = jnp.sum(x * x, -1, keepdims=True)
            return 2.0 / jnp.clip(1.0 - c * x2, MIN_NORM, None)

        def expmap(u, p, c):
            sc = jnp.sqrt(c)
            un = _norm(u)
            second = jnp.tanh(0.5 * sc * lambda_x(p, c) * un) * u / (sc * un)
            return mobius_add(p, second, c)

        def logmap(p1, p2, c):
            sub = mobius_add(-p1, p2, c)
            sn = _norm(sub)
            sc = jnp.sqrt(c)
            return 2.0 / (sc * lambda_x(p1, c)) * artanh(sc * sn) * sub / sn

        def mobius_matvec(m, x, c):
            sc = jnp.sqrt(c)
            xn = _norm(x)
            mx = x @ m.T
            mxn = _norm(mx)
            res = jnp.tanh(mxn / xn * artanh(sc * xn)) * mx / (mxn * sc)
            zero_row = jnp.all(mx == 0, axis=-1, keepdims=True)
            return jnp.where(zero_row, jnp.zeros_like(res), res)
        c = C
        b, n, d = x.shape
        h = proj(mobius_matvec(W, x, c), c)
        hyp_bias = proj(expmap0(b_lin[None, None, :], c), c)
        h = proj(mobius_add(h, hyp_bias, c), c)
        x_provide = jnp.broadcast_to(h[:, :, None, :], (b, n, n, d))
        x_map = jnp.broadcast_to(h[:, None, :, :], (b, n, n, d))
        x_loc = jnp.clip(logmap(x_provide, x_map, c), -1000.0, 1000.0)
        x_self = logmap(h, h, c)
        q = jnp.concatenate([jnp.broadcast_to(x_self[:, :, None, :], (b, n, n, d)), x_loc], axis=-1)
        a = jax.nn.silu(q @ att_w1.T + att_b1)
        adj_att = jax.nn.sigmoid(a @ att_w2.T + att_b2)[..., 0]
        support_t = jnp.sum(adj_att[..., None] * x_loc * mask[..., None], axis=2)
        t = jnp.concatenate([x_self, support_t], axis=-1)
        support_t = jax.nn.silu(t @ mlp_w1.T + mlp_b1) @ mlp_w2.T + mlp_b2 + x_self
        out = proj(expmap(support_t, h, c), c)
        xt = jax.nn.silu(logmap0(out, c))
        out = proj(expmap0(xt, c), c)
        return out

    def _L2_gnn_ref(x, adj, W, b):
        import jax, jax.numpy as jnp
        import numpy as np
        B, N, DIN, DOUT = (8, 2048, 128, 128)
        degree = jnp.sum(adj, axis=2)
        d_norm = 1.0 / jnp.sqrt(degree + 1e-08)
        adj_norm = d_norm[:, :, None] * adj * d_norm[:, None, :]
        support = jnp.einsum('bnm,bmd->bnd', adj_norm, x)
        return support @ W + b

    def _L3_gnn_ref(x, adj, W_msg, W_upd):
        import jax, jax.numpy as jnp
        import numpy as np
        UNITS = 128
        D_FEAT = 128
        B, N = (4, 4096)
        EDGE_PROB = 0.01
        d = x.shape[-1]
        Ws, Wr = (W_msg[:d], W_msg[d:])
        xs = x @ Ws
        xr = x @ Wr
        deg = jnp.einsum('bsr->br', adj)[..., None]
        snd_sum = jnp.einsum('bsr,bsu->bru', adj, xs)
        messages = jnp.where(deg > 0, snd_sum / jnp.maximum(deg, 1.0) + xr, 0.0)
        return jnp.concatenate([x, messages], axis=-1) @ W_upd

    h = jnp.maximum(_layernorm(x, axis=-1), 0.0)
    x = x + _L0_gnn_ref(h, adj, adj, L0_gnn_W1, L0_gnn_b1, L0_gnn_W2, L0_gnn_b2, L0_gnn_Wa, L0_gnn_Wd1, L0_gnn_bd1, L0_gnn_Wd2, L0_gnn_bd2)
    h = jnp.maximum(_layernorm(x, axis=-1), 0.0)
    x = x + _L1_gnn_ref(h, adj, L1_gnn_W, L1_gnn_b_lin, L1_gnn_att_w1, L1_gnn_att_b1, L1_gnn_att_w2, L1_gnn_att_b2, L1_gnn_mlp_w1, L1_gnn_mlp_b1, L1_gnn_mlp_w2, L1_gnn_mlp_b2)
    h = jnp.maximum(_layernorm(x, axis=-1), 0.0)
    x = x + _L2_gnn_ref(h, adj, L2_gnn_W, L2_gnn_b)
    h = jnp.maximum(_layernorm(x, axis=-1), 0.0)
    x = x + _L3_gnn_ref(h, adj, L3_gnn_W_msg, L3_gnn_W_upd)
    return x


_drawn_inputs = setup_inputs


def setup_inputs(seed=0):
    import zlib

    import numpy as np

    out = dict(_drawn_inputs(seed))
    spreads = {'L0_gnn_b1': (0.0, 0.1),
     'L0_gnn_b2': (0.0, 0.1),
     'L0_gnn_bd1': (0.0, 0.1),
     'L0_gnn_bd2': (0.0, 0.1),
     'L1_gnn_b_lin': (0.0, 0.8),
     'L1_gnn_att_b1': (0.0, 0.8),
     'L1_gnn_mlp_b1': (0.0, 0.8),
     'L1_gnn_mlp_b2': (0.0, 0.8)}
    factors = {'L1_gnn_att_w1': 8.0,
     'L1_gnn_att_w2': 8.0,
     'L1_gnn_mlp_w1': 8.0,
     'L1_gnn_mlp_w2': 8.0,
     'L2_gnn_b': 6.72}
    for name, (base, spread) in spreads.items():
        noise = np.random.default_rng([zlib.crc32(name.encode()), seed]).standard_normal(out[name].shape)
        drawn = base * np.exp(spread * noise) if base else spread * noise
        out[name] = jnp.asarray(drawn.astype(out[name].dtype))
    for name, factor in factors.items():
        out[name] = (out[name] * factor).astype(out[name].dtype)
    return out
```

```python
from contextlib import ExitStack

import concourse.bass as bass
import numpy as np
from concourse import mybir

F32 = mybir.dt.float32
I32 = mybir.dt.int32
ALU = mybir.AluOpType
ACT = mybir.ActivationFunctionType
AX = mybir.AxisListType.X

P = 128
GRAPHS, NODES = 128, 64
NG = 64
CUTOFF = 5.0
TILES = GRAPHS // 2
PAIRS = NODES * NODES
GT = 8
GROUPS = TILES // GT
BANK = 512
LN2 = float(np.log(2.0))
OFFSETS = np.linspace(0.0, CUTOFF, NG, dtype=np.float32)
COEFF = float(np.float32(-0.5) / ((OFFSETS[1] - OFFSETS[0]) * (OFFSETS[1] - OFFSETS[0])))
EXP_CAP = 2.0 ** 60
MIN_NORM = 1e-15
MAX_NORM = 1.0 - 0.004
ONE_LESS = 1.0 - 1e-7
SMALL_SQ = 1.0 / 64
LN_EPS = 1e-5


class Chain:

    def __init__(self, sem):
        self.sem, self.base, self.k, self.turn, self.per = sem, 0, 0, None, 0

    def value(self):
        v = self.base + self.k
        return v if self.turn is None else self.turn * self.per + v

    def step(self, engine, emit):
        v = self.value()
        if not (isinstance(v, int) and v == 0):
            engine.wait_ge(self.sem, v)
        emit().then_inc(self.sem, 1)
        self.k += 1

    def loop(self, nc, turns, per, body):
        self.base, self.k = self.base + self.k, 0
        with nc.Fori(0, turns) as turn:
            self.turn, self.per = turn, per
            body(turn)
            assert self.k == per, (self.k, per)
        self.base, self.k, self.turn = self.base + turns * per, 0, None


def build(nc, t, out):
    V, A, PE, GP, SP = nc.vector, nc.scalar, nc.tensor, nc.gpsimd, nc.sync
    ctx = ExitStack()
    with ctx:
        def sem(name):
            return ctx.enter_context(nc.semaphore(name))

        def sb(name, shape, dt=F32, where=ctx):
            return where.enter_context(nc.sbuf_tensor(name, shape, dt))

        def dram(name, shape):
            return nc.dram_tensor(name, shape, F32, kind="Internal").ap()

        PS = ctx.enter_context(nc.psum_tensor("PS", [P, 8, BANK], F32))

        def tiles(ap):
            return ap.rearrange("(t p) d -> p t d", p=P)

        x_in = tiles(t["x"].rearrange("b n d -> (b n) d"))
        x_out = tiles(out.rearrange("b n d -> (b n) d"))
        adj_pairs = t["adj"].rearrange("b i j -> b (i j)")
        adj_rows = tiles(t["adj"].rearrange("b i j -> (b i) j"))
        adjT_rows = tiles(t["adjT"].rearrange("b j i -> (b j) i"))
        adj_sq = dram("adj_sq", [GRAPHS, PAIRS])
        x1_d = dram("x1_d", [GRAPHS * NODES, P])
        h_d = dram("h_d", [GRAPHS * NODES, P])
        hw_d = dram("hw_d", [GRAPHS * NODES, P])
        hs_d = dram("hs_d", [GRAPHS * NODES, P])
        att_d = dram("att_d", [GRAPHS * NODES, NODES])

        chain = Chain(sem("chain"))
        s_load, s_store = sem("s_load"), sem("s_store")
        loads = Chain(s_load)
        stores = Chain(s_store)

        def v(emit): chain.step(V, emit)
        def a(emit): chain.step(A, emit)
        def pe(emit): chain.step(PE, emit)
        def gp(emit): chain.step(GP, emit)

        def dma(sm, count, pairs):
            def go():
                for dst, src in pairs:
                    SP.dma_start(dst, src).then_inc(sm, 16)
                SP.wait_ge(sm, count)
                return SP.nop()
            chain.step(SP, go)

        apart = sem("apart")
        dma_done = [0, 0]

        def transfer(kind, pairs, turn=None, per=0):
            dma_done[kind] += 16 * len(pairs)
            count = dma_done[kind] if turn is None else turn * per + dma_done[kind]
            dma((s_load, s_store)[kind], count, pairs)

        def const(name, shape):
            return sb(name, shape)

        W = {n: const("w_" + n, [P, P]) for n in
             ("WaT", "W2T", "Wd1T", "Wd2T", "WT", "Wm1LT", "Wm1RT", "Wm2T", "Wg", "Wmsg_s", "Wmsg_r", "Wub", "WsT", "WrT")}
        WrlT = const("WrlT", [P, 2 * P])
        W3 = const("W3", [P, 3 * P])
        W1pad = const("W1pad", [P, 2, P])
        w2sel = const("w2sel", [P, 64])
        cols = {n: const("c_" + n, [P, 1]) for n in
                ("b1", "b1l", "b2", "bd1", "bd1l", "att_b1", "mlp_b1", "att_w2", "att_b2", "off", "hb2")}
        rows = {n: const("r_" + n, [P, P]) for n in ("bd2", "hb", "mlp_b2", "L2_b")}
        ident = const("ident", [P, P])
        ones = const("ones", [P, NODES])
        rfT = sb("rfT", [P, TILES * P])
        x2_all = const("x2_all", [P, TILES])
        cs_all = const("cs_all", [P, TILES])
        small = const("small", [P, 40, GT])
        tmpc = const("tmpc", [P, 8])
        off_i = sb("off_i", [P, 1], I32)

        gp(lambda: GP.memset(ident[:], 0.0))
        gp(lambda: GP.affine_select(out=ident[:], in_=ident[:], compare_op=ALU.not_equal, fill=1.0,
                                    base=0, pattern=[[-1, P]], channel_multiplier=1))
        gp(lambda: GP.memset(ones[:], 1.0))
        gp(lambda: GP.memset(W1pad[:], 0.0))
        gp(lambda: GP.memset(w2sel[:], 0.0))
        gp(lambda: GP.iota(off_i[0:NG, :], [[0, 1]], base=0, channel_multiplier=1))
        gp(lambda: GP.iota(off_i[NG:P, :], [[0, 1]], base=0, channel_multiplier=1))

        def column(ap):
            return ap.rearrange("(p o) -> p o", o=1)

        def across(ap):
            return ap.rearrange("(o n) -> o n", o=1).broadcast_to([P, ap.shape[0]])

        transfer(0, [
            (W["WaT"][:], t["WaT"]), (W["W2T"][:], t["W2T"]), (W["Wd1T"][:], t["Wd1T"]),
            (W["Wd2T"][:], t["Wd2T"]), (W["WT"][:], t["WT"]), (W["Wm2T"][:], t["Wm2T"]),
            (W["Wm1LT"][:], t["Wm1T"][0:P, :]), (W["Wm1RT"][:], t["Wm1T"][P:2 * P, :]),
            (W["Wg"][:], t["L2_gnn_W"]),
            (W["Wmsg_s"][:], t["L3_gnn_W_msg"][0:P, :]), (W["Wmsg_r"][:], t["L3_gnn_W_msg"][P:2 * P, :]),
            (W["Wub"][:], t["L3_gnn_W_upd"][P:2 * P, :]), (W3[:, P:2 * P], t["L3_gnn_W_upd"][0:P, :]),
            (WrlT[:, 0:P], t["WattT"][P:2 * P, :]), (WrlT[:, P:2 * P], t["WattT"][0:P, :]),
            (W1pad[0:NG, 0, :], t["W1T"]), (W1pad[NG:P, 1, :], t["W1T"]),
            (cols["b1"][:], column(t["L0_gnn_b1"])), (cols["b2"][:], column(t["L0_gnn_b2"])),
            (cols["bd1"][:], column(t["L0_gnn_bd1"])), (cols["att_b1"][:], column(t["L1_gnn_att_b1"])),
            (cols["mlp_b1"][:], column(t["L1_gnn_mlp_b1"])),
            (cols["att_w2"][:], t["L1_gnn_att_w2"].rearrange("o p -> p o")),
            (cols["att_b2"][:], across(t["L1_gnn_att_b2"])),
            (rows["bd2"][:], across(t["L0_gnn_bd2"])), (rows["hb"][:], across(t["L1_gnn_b_lin"])),
            (rows["mlp_b2"][:], across(t["L1_gnn_mlp_b2"])), (rows["L2_b"][:], across(t["L2_gnn_b"])),
        ])
        v(lambda: V.tensor_copy(w2sel[:, 32:33], cols["att_w2"][:]))
        v(lambda: V.tensor_copy(cols["off"][:], off_i[:]))
        v(lambda: V.tensor_scalar(cols["off"][:], cols["off"][:], -CUTOFF, 1.0 / (NG - 1), ALU.mult, ALU.mult))
        v(lambda: V.tensor_scalar(cols["b1l"][:], cols["b1"][:], -LN2, None, ALU.add))
        v(lambda: V.tensor_scalar(cols["bd1l"][:], cols["bd1"][:], -LN2, None, ALU.add))
        v(lambda: V.tensor_scalar(cols["att_b2"][:], cols["att_b2"][:], 0.5, None, ALU.mult))

        pe(lambda: PE.transpose(PS[:, 0, 0:P], W["Wmsg_s"][:], ident[:]))
        pe(lambda: PE.transpose(PS[:, 1, 0:P], W["Wmsg_r"][:], ident[:]))
        v(lambda: V.tensor_copy(W["WsT"][:], PS[:, 0, 0:P]))
        v(lambda: V.tensor_copy(W["WrT"][:], PS[:, 1, 0:P]))
        pe(lambda: PE.matmul(PS[:, 0, 0:P], W["WsT"][:], W["Wub"][:], start=True, stop=True))
        pe(lambda: PE.matmul(PS[:, 1, 0:P], W["WrT"][:], W["Wub"][:], start=True, stop=True))
        v(lambda: V.tensor_copy(W3[:, 0:P], PS[:, 0, 0:P]))
        v(lambda: V.tensor_copy(W3[:, 2 * P:3 * P], PS[:, 1, 0:P]))

        def ts(o, i, s1, op0, s2=None, op1=None):
            if op1 is None:
                v(lambda: V.tensor_scalar(o, i, s1, None, op0))
            else:
                v(lambda: V.tensor_scalar(o, i, s1, s2, op0, op1))

        def tt(o, x, y, op):
            v(lambda: V.tensor_tensor(o, x, y, op))

        def stt(o, x, s, y, op0, op1):
            v(lambda: V.scalar_tensor_tensor(o, x, s, y, op0, op1))

        def recip(o, i):
            v(lambda: V.reciprocal(o, i))

        def act(o, i, f, scale=1.0, bias=0.0):
            a(lambda: A.activation(o, i, f, bias=bias, scale=scale))

        def rsum(o, i):
            v(lambda: V.tensor_reduce(o, i, AX, ALU.add))

        def series(o, q):
            ts(o, q, 1.0 / 11, ALU.mult)
            for d in (9, 7, 5, 3):
                stt(o, o, 1.0 / d, q, ALU.add, ALU.mult)
            ts(o, o, 1.0, ALU.add)

        def artanh_over(o, q, z, ratio, m, w):
            act(w, ratio, ACT.Ln)
            ts(m, z, 0.1, ALU.max)
            recip(m, m)
            stt(w, w, 0.5, m, ALU.mult, ALU.mult)
            series(o, q)
            tt(w, w, o, ALU.subtract)
            ts(m, q, SMALL_SQ, ALU.is_ge)
            tt(w, w, m, ALU.mult)
            tt(o, o, w, ALU.add)

        def artanh(o, z, q, ratio, m, w):
            ts(m, z, -1.0, ALU.mult, 1.0, ALU.add)
            recip(m, m)
            stt(ratio, z, 1.0, m, ALU.add, ALU.mult)
            tt(q, z, z, ALU.mult)
            artanh_over(o, q, z, ratio, m, w)
            tt(o, o, z, ALU.mult)

        with ExitStack() as c0:
            sq = sb("sq0", [P, P], where=c0)
            tt(sq[:], rows["hb"][:], rows["hb"][:], ALU.mult)
            rsum(tmpc[:, 0:1], sq[:])
            act(tmpc[:, 1:2], tmpc[:, 0:1], ACT.Sqrt)
            ts(tmpc[:, 1:2], tmpc[:, 1:2], MIN_NORM, ALU.max)
            recip(tmpc[:, 2:3], tmpc[:, 1:2])
            act(tmpc[:, 3:4], tmpc[:, 1:2], ACT.Tanh)
            ts(tmpc[:, 3:4], tmpc[:, 3:4], MAX_NORM, ALU.min)
            tt(tmpc[:, 3:4], tmpc[:, 3:4], tmpc[:, 2:3], ALU.mult)
            ts(rows["hb"][:], rows["hb"][:], tmpc[:, 3:4], ALU.mult)
            tt(sq[:], rows["hb"][:], rows["hb"][:], ALU.mult)
            rsum(cols["hb2"][:], sq[:])

            ad = sb("ad", [P, PAIRS], where=c0)
            transfer(0, [(ad[:], adj_pairs)])
            tt(ad[:], ad[:], ad[:], ALU.mult)
            transfer(1, [(adj_sq, ad[:])])

        def bc(col):
            return col.unsqueeze(2).broadcast_to([P, GT, P])

        def brow(row):
            return row[:].unsqueeze(1).broadcast_to([P, GT, P])

        def flat(buf):
            return buf[:].rearrange("p t d -> p (t d)")

        def S(n):
            return small[:, n, :]

        def bank2(n):
            return PS[:, n:n + 2, :].rearrange("p b (t d) -> p (b t) d", d=P)

        def bankf(n):
            return PS[:, n:n + 2, :].rearrange("p b n -> p (b n)")

        def norm_relu(X, XC, SQ, H, extra=None):
            rsum(S(0), X[:])
            ts(S(0), S(0), 1.0 / P, ALU.mult)
            tt(XC[:], X[:], bc(S(0)), ALU.subtract)
            tt(SQ[:], XC[:], XC[:], ALU.mult)
            rsum(S(1), SQ[:])
            ts(S(1), S(1), 1.0 / P, ALU.mult, LN_EPS, ALU.add)
            act(S(1), S(1), ACT.Sqrt)
            recip(S(1), S(1))
            if extra is not None:
                tt(S(1), S(1), extra, ALU.mult)
            stt(H[:], XC[:], 0.0, bc(S(1)), ALU.max, ALU.mult)

        def turn_tiles(SRC, bank, DST):
            def go():
                for k in range(GT):
                    last = PE.transpose(bank2(bank)[:, k, :], SRC[:, k, :], ident[:])
                return last
            pe(go)
            act(flat(DST), bankf(bank), ACT.Copy)

        def wide(bank, parts):
            def go():
                for c in range(2):
                    for n, (w, cols_of) in enumerate(parts):
                        last = PE.matmul(PS[:, bank + c, :], w, cols_of(c), start=n == 0, stop=n == len(parts) - 1)
                return last
            pe(go)

        def half(buf):
            return lambda c: flat(buf)[:, c * BANK:(c + 1) * BANK]

        def per_tile(bank, lhs, rhs, width=P):
            region = PS[:, bank:bank + 2 * width // P, :].rearrange("p b n -> p (b n)")
            def go():
                for k in range(GT):
                    last = PE.matmul(region[:, k * width:(k + 1) * width], lhs(k), rhs(k), start=True, stop=True)
                return last
            pe(go)
            return region

        def ssp(o, i, bias, bias_l):
            act(o, i, ACT.Exp, bias=bias)
            ts(o, o, EXP_CAP, ALU.min)
            act(o, o, ACT.Ln, scale=0.5, bias=half_col[:])
            stt(o, i, bias_l, o, ALU.add, ALU.max)

        half_col = const("half_col", [P, 1])
        v(lambda: V.memset(half_col[:], 0.5))

        def squares(o, X, Y, SQ):
            tt(SQ[:], X[:] if X is not None else None, Y[:], ALU.mult)
            rsum(o, SQ[:])

        with ExitStack() as c1:
            X, XC, SQ, H, HT = (sb(n + "1", [P, GT, P], where=c1) for n in ("X", "XC", "SQ", "H", "HT"))
            base = dma_done[0]

            def prepare(g):
                transfer(0, [(X[:], x_in[:, bass.ds(g * GT, GT), :])], g, 16)
                norm_relu(X, XC, SQ, H)
                turn_tiles(H, 0, HT)
                wide(2, [(W["WaT"][:], half(HT))])
                act(rfT[:, bass.ds(g * (GT * P), GT * P)], bankf(2), ACT.Copy)

            chain.loop(nc, GROUPS, 14, prepare)
            dma_done[0] = base + 16 * GROUPS
        nc.all_engine_barrier()

        c2 = ExitStack()
        with c2:
            yT = sb("yT", [P, TILES * P], where=ctx)
            filter_stage(nc, ctx, c2, PS, apart, adj_pairs, adj_sq, rfT, yT, W1pad, W["W2T"], cols, half_col)
        nc.all_engine_barrier()

        pair = {n: sb("pair_" + n, [P, TILES, NODES]) for n in ("U", "VT", "VP")}
        with ExitStack() as c3:
            X, XC, SQ, H, HT, MX, HQ = (sb(n + "3", [P, GT, P], where=c3)
                                        for n in ("X", "XC", "SQ", "H", "HT", "MX", "HQ"))
            q5 = {n: sb("q5" + n, [P, GT, NODES], where=c3) for n in ("y2", "a1", "den", "n1", "q", "z", "r", "m", "w", "T", "oy")}
            base = list(dma_done)

            def between(g):
                nodes = bass.ds(g * GT, GT)
                transfer(0, [(X[:], x_in[:, nodes, :])], g, 16)
                pe(lambda: [PE.matmul(PS[:, c, :], W["Wd1T"][:], yT[:, bass.ds(g * (GT * P) + c * BANK, BANK)],
                                      start=True, stop=True) for c in range(2)][-1])
                ssp(flat(HT), bankf(0), cols["bd1"][:], cols["bd1l"][:])
                per_tile(2, lambda k: HT[:, k, :], lambda k: W["Wd2T"][:])
                tt(X[:], bank2(2), X[:], ALU.add)
                tt(X[:], X[:], brow(rows["bd2"]), ALU.add)
                transfer(1, [(tiles(x1_d)[:, nodes, :], X[:])], g, 16 * 4)
                norm_relu(X, XC, SQ, H)
                turn_tiles(H, 0, HT)
                per_tile(2, lambda k: HT[:, k, :], lambda k: W["WT"][:])
                act(flat(MX), bankf(2), ACT.Copy)
                squares(S(2), H, H, SQ)
                squares(S(3), MX, MX, SQ)
                tt(SQ[:], MX[:], brow(rows["hb"]), ALU.mult)
                rsum(S(4), SQ[:])
                act(S(5), S(2), ACT.Sqrt)
                act(S(6), S(3), ACT.Sqrt)
                ts(S(5), S(5), MIN_NORM, ALU.max)
                ts(S(6), S(6), MIN_NORM, ALU.max)
                ts(S(7), S(5), ONE_LESS, ALU.min)
                artanh(S(8), S(7), S(9), S(10), S(11), S(12))
                recip(S(13), S(5))
                recip(S(14), S(6))
                tt(S(8), S(8), S(13), ALU.mult)
                tt(S(8), S(8), S(6), ALU.mult)
                act(S(8), S(8), ACT.Tanh)
                ts(S(8), S(8), MAX_NORM, ALU.min)
                tt(S(8), S(8), S(14), ALU.mult)
                tt(S(15), S(8), S(8), ALU.mult)
                tt(S(15), S(15), S(3), ALU.mult)
                tt(S(16), S(8), S(4), ALU.mult)
                ts(S(16), S(16), 2.0, ALU.mult, 1.0, ALU.add)
                ts(S(17), S(15), cols["hb2"][:], ALU.mult)
                tt(S(17), S(17), S(16), ALU.add)
                ts(S(17), S(17), MIN_NORM, ALU.max)
                recip(S(17), S(17))
                ts(S(16), S(16), cols["hb2"][:], ALU.add)
                tt(S(16), S(16), S(8), ALU.mult)
                tt(S(16), S(16), S(17), ALU.mult)
                ts(S(15), S(15), -1.0, ALU.mult, 1.0, ALU.add)
                tt(S(15), S(15), S(17), ALU.mult)
                tt(H[:], MX[:], bc(S(16)), ALU.mult)
                tt(SQ[:], brow(rows["hb"]), bc(S(15)), ALU.mult)
                tt(H[:], H[:], SQ[:], ALU.add)
                squares(S(18), H, H, SQ)
                act(S(19), S(18), ACT.Sqrt)
                ts(S(19), S(19), MIN_NORM, ALU.max)
                recip(S(19), S(19))
                ts(S(19), S(19), MAX_NORM, ALU.mult, 1.0, ALU.min)
                tt(H[:], H[:], bc(S(19)), ALU.mult)
                squares(S(20), H, H, SQ)
                v(lambda: V.tensor_copy(x2_all[:, nodes], S(20)))
                ts(S(21), S(20), -1.0, ALU.mult, 1.0, ALU.add)
                ts(S(22), S(20), -2.0, ALU.mult, 1.0, ALU.add)
                tt(S(23), S(22), S(20), ALU.add)
                tt(S(23), S(21), S(23), ALU.subtract)
                tt(S(24), S(20), S(20), ALU.mult)
                tt(S(24), S(24), S(22), ALU.add)
                recip(S(24), S(24))
                tt(S(23), S(23), S(24), ALU.mult)
                tt(S(24), S(23), S(23), ALU.mult)
                tt(S(24), S(24), S(20), ALU.mult)
                series(S(25), S(24))
                tt(S(25), S(25), S(23), ALU.mult)
                tt(S(25), S(25), S(21), ALU.mult)
                v(lambda: V.tensor_copy(cs_all[:, nodes], S(25)))
                turn_tiles(H, 0, HT)
                r = per_tile(4, lambda k: HT[:, k, :], lambda k: WrlT[:], 2 * P)
                r = r.rearrange("p (t w) -> p t w", w=2 * P)
                act(XC[:], r[:, :, 0:P], ACT.Copy)
                tt(SQ[:], r[:, :, P:2 * P], bc(S(25)), ALU.mult)
                transfer(1, [(tiles(h_d)[:, nodes, :], H[:]), (tiles(hw_d)[:, nodes, :], XC[:]),
                             (tiles(hs_d)[:, nodes, :], SQ[:])], g, 16 * 4)
                tt(HQ[:], HT[:], HT[:], ALU.mult)

                def dots():
                    for k in range(GT):
                        for b in range(2):
                            rows_of = slice(b * NODES, (b + 1) * NODES)
                            PE.matmul(PS[rows_of, 0, k * NODES:(k + 1) * NODES], HT[:, k, rows_of], HT[:, k, rows_of],
                                      start=True, stop=True)
                            last = PE.matmul(PS[rows_of, 1, k * NODES:(k + 1) * NODES], ones[:], HQ[:, k, rows_of],
                                             start=True, stop=True)
                    return last
                pe(dots)
                G = PS[:, 0, :].rearrange("p (t j) -> p t j", j=NODES)
                Y2 = PS[:, 1, :].rearrange("p (t j) -> p t j", j=NODES)

                def nc_(col):
                    return col.unsqueeze(2).broadcast_to([P, GT, NODES])
                act(q5["y2"][:], Y2, ACT.Copy)
                ts(q5["a1"][:], G, -2.0, ALU.mult, 1.0, ALU.add)
                tt(q5["den"][:], q5["y2"][:], nc_(S(20)), ALU.mult)
                tt(q5["den"][:], q5["den"][:], q5["a1"][:], ALU.add)
                ts(q5["den"][:], q5["den"][:], MIN_NORM, ALU.max)
                tt(q5["n1"][:], q5["a1"][:], q5["y2"][:], ALU.add)
                stt(q5["q"][:], G, -2.0, q5["y2"][:], ALU.mult, ALU.add)
                tt(q5["q"][:], q5["q"][:], nc_(S(20)), ALU.add)
                recip(q5["T"][:], q5["den"][:])
                stt(q5["q"][:], q5["q"][:], 0.0, q5["T"][:], ALU.max, ALU.mult)
                act(q5["z"][:], q5["q"][:], ACT.Sqrt)
                ts(q5["oy"][:], q5["y2"][:], -1.0, ALU.mult, 1.0, ALU.add)
                tt(q5["m"][:], q5["oy"][:], nc_(S(21)), ALU.mult)
                recip(q5["m"][:], q5["m"][:])
                tt(q5["m"][:], q5["m"][:], q5["den"][:], ALU.mult)
                stt(q5["r"][:], q5["z"][:], 1.0, q5["m"][:], ALU.add, ALU.mult)
                stt(q5["r"][:], q5["z"][:], 1.0, q5["r"][:], ALU.add, ALU.mult)
                v(lambda: V.tensor_copy(q5["a1"][:], q5["T"][:]))
                artanh_over(q5["T"][:], q5["q"][:], q5["z"][:], q5["r"][:], q5["m"][:], q5["w"][:])
                tt(q5["T"][:], q5["T"][:], q5["a1"][:], ALU.mult)
                tt(q5["m"][:], q5["oy"][:], q5["oy"][:], ALU.mult)
                tt(pair["VT"][:, nodes, :], q5["m"][:], q5["T"][:], ALU.mult)
                tt(q5["m"][:], q5["T"][:], nc_(S(21)), ALU.mult)
                tt(pair["VP"][:, nodes, :], q5["m"][:], nc_(S(21)), ALU.mult)
                stt(pair["U"][:, nodes, :], q5["m"][:], -1.0, q5["n1"][:], ALU.mult, ALU.mult)

            chain.loop(nc, GROUPS, BETWEEN_STEPS, between)
            dma_done[0] = base[0] + 16 * GROUPS
            dma_done[1] = base[1] + 16 * 4 * GROUPS
        nc.all_engine_barrier()

        with ExitStack() as c4:
            attend_stage(nc, ctx, c4, PS, apart, hw_d, hs_d, att_d, pair["U"], pair["VT"], w2sel, cols)
        nc.all_engine_barrier()

        with ExitStack() as c5:
            X, XC, SQ, H, HT, ST, UU, AV, AVT, AB, ABT = (
                sb(n + "5", [P, GT, P], where=c5)
                for n in ("X", "XC", "SQ", "H", "HT", "ST", "UU", "AV", "AVT", "AB", "ABT"))
            at, am, sc = (sb(n + "5", [P, GT, NODES], where=c5) for n in ("at", "am", "sc"))
            for buf in (AV, AB, ABT):
                v(lambda buf=buf: V.memset(buf[:], 0.0))
            base = list(dma_done)

            def two_blocks(buf):
                return [(slice(0, NODES), buf[0:NODES, :, 0:NODES]), (slice(NODES, P), buf[NODES:P, :, NODES:P])]

            def finish(g):
                nodes = bass.ds(g * GT, GT)
                transfer(0, [(X[:], tiles(x1_d)[:, nodes, :]), (H[:], tiles(h_d)[:, nodes, :]),
                             (at[:], tiles(att_d)[:, nodes, :]), (am[:], adj_rows[:, nodes, :])]
                         + [(blk, adj_rows[r, nodes, :]) for r, blk in two_blocks(AB)]
                         + [(blk, adjT_rows[r, nodes, :]) for r, blk in two_blocks(ABT)], g, 16 * 8)
                ts(at[:], at[:], 0.5, ALU.mult, 0.5, ALU.add)
                tt(am[:], am[:], at[:], ALU.mult)
                tt(sc[:], am[:], pair["U"][:, nodes, :], ALU.mult)
                rsum(S(0), sc[:])
                for r, blk in two_blocks(AV):
                    tt(blk, am[r, :, :], pair["VP"][r, nodes, :], ALU.mult)
                v(lambda: [V.scalar_tensor_tensor(AV[:, k, :], ident[:], small[:, 0, k:k + 1], AV[:, k, :],
                                                  ALU.mult, ALU.add) for k in range(GT)][-1])
                turn_tiles(AV, 0, AVT)
                per_tile(2, lambda k: H[:, k, :], lambda k: AVT[:, k, :])
                act(flat(ST), bankf(2), ACT.Copy)
                tt(UU[:], H[:], bc(cs_all[:, nodes]), ALU.mult)
                turn_tiles(UU, 0, HT)
                wide(2, [(W["Wm1LT"][:], half(HT)), (W["Wm1RT"][:], half(ST))])
                act(flat(ST), bankf(2), ACT.Silu, bias=cols["mlp_b1"][:])
                per_tile(0, lambda k: ST[:, k, :], lambda k: W["Wm2T"][:])
                tt(UU[:], bank2(0), UU[:], ALU.add)
                tt(UU[:], UU[:], brow(rows["mlp_b2"]), ALU.add)
                squares(S(1), UU, UU, SQ)
                squares(S(2), H, UU, SQ)
                v(lambda: V.tensor_copy(S(3), x2_all[:, nodes]))
                ts(S(4), S(3), -1.0, ALU.mult, 1.0, ALU.add)
                act(S(5), S(1), ACT.Sqrt)
                ts(S(5), S(5), MIN_NORM, ALU.max)
                ts(S(6), S(4), MIN_NORM, ALU.max)
                recip(S(6), S(6))
                tt(S(6), S(6), S(5), ALU.mult)
                act(S(6), S(6), ACT.Tanh)
                recip(S(7), S(5))
                tt(S(6), S(6), S(7), ALU.mult)
                tt(S(8), S(6), S(6), ALU.mult)
                tt(S(8), S(8), S(1), ALU.mult)
                tt(S(9), S(6), S(2), ALU.mult)
                ts(S(9), S(9), 2.0, ALU.mult, 1.0, ALU.add)
                tt(S(10), S(8), S(3), ALU.mult)
                tt(S(10), S(10), S(9), ALU.add)
                ts(S(10), S(10), MIN_NORM, ALU.max)
                recip(S(10), S(10))
                tt(S(9), S(9), S(8), ALU.add)
                tt(S(9), S(9), S(10), ALU.mult)
                tt(S(4), S(4), S(6), ALU.mult)
                tt(S(4), S(4), S(10), ALU.mult)
                tt(H[:], H[:], bc(S(9)), ALU.mult)
                tt(UU[:], UU[:], bc(S(4)), ALU.mult)
                tt(H[:], H[:], UU[:], ALU.add)
                squares(S(11), H, H, SQ)
                act(S(12), S(11), ACT.Sqrt)
                ts(S(13), S(12), MIN_NORM, ALU.max)
                recip(S(14), S(13))
                ts(S(14), S(14), MAX_NORM, ALU.mult, 1.0, ALU.min)
                tt(S(15), S(13), S(14), ALU.mult)
                ts(S(15), S(15), MIN_NORM, ALU.max)
                ts(S(16), S(15), ONE_LESS, ALU.min)
                artanh(S(17), S(16), S(18), S(19), S(20), S(21))
                recip(S(15), S(15))
                tt(S(17), S(17), S(15), ALU.mult)
                tt(S(17), S(17), S(14), ALU.mult)
                tt(H[:], H[:], bc(S(17)), ALU.mult)
                act(H[:], H[:], ACT.Silu)
                squares(S(22), H, H, SQ)
                act(S(23), S(22), ACT.Sqrt)
                ts(S(23), S(23), MIN_NORM, ALU.max)
                recip(S(24), S(23))
                act(S(23), S(23), ACT.Tanh)
                ts(S(23), S(23), MAX_NORM, ALU.min)
                tt(S(23), S(23), S(24), ALU.mult)
                tt(H[:], H[:], bc(S(23)), ALU.mult)
                tt(X[:], X[:], H[:], ALU.add)
                rsum(S(25), AB[:])
                ts(S(25), S(25), 1e-8, ALU.add)
                act(S(25), S(25), ACT.Sqrt)
                recip(S(25), S(25))
                norm_relu(X, XC, SQ, H, extra=S(25))
                per_tile(0, lambda k: H[:, k, :], lambda k: ABT[:, k, :])
                act(flat(ST), bankf(0), ACT.Copy)
                per_tile(2, lambda k: ST[:, k, :], lambda k: W["Wg"][:])
                tt(SQ[:], bank2(2), bc(S(25)), ALU.mult)
                tt(X[:], X[:], SQ[:], ALU.add)
                tt(X[:], X[:], brow(rows["L2_b"]), ALU.add)
                norm_relu(X, XC, SQ, H)
                turn_tiles(H, 0, HT)
                rsum(S(26), ABT[:])
                ts(S(27), S(26), 0.0, ALU.is_gt)
                ts(S(26), S(26), 1.0, ALU.max)
                recip(S(26), S(26))
                tt(S(26), S(26), S(27), ALU.mult)

                def three():
                    for k in range(GT // 2, GT):
                        last = PE.matmul(PS[:, k, 0:3 * P], HT[:, k, :], W3[:], start=True, stop=True)
                    return last

                def three_low():
                    for k in range(GT // 2):
                        last = PE.matmul(PS[:, k, 0:3 * P], HT[:, k, :], W3[:], start=True, stop=True)
                    return last
                pe(three_low)
                pe(three)
                act(XC[:], PS[:, :, 0:P], ACT.Copy)
                tt(X[:], PS[:, :, P:2 * P], X[:], ALU.add)
                tt(SQ[:], PS[:, :, 2 * P:3 * P], bc(S(27)), ALU.mult)
                tt(X[:], X[:], SQ[:], ALU.add)
                per_tile(0, lambda k: AB[:, k, :], lambda k: XC[:, k, :])
                tt(SQ[:], bank2(0), bc(S(26)), ALU.mult)
                tt(X[:], X[:], SQ[:], ALU.add)
                transfer(1, [(x_out[:, nodes, :], X[:])], g, 16)

            chain.loop(nc, GROUPS, FINISH_STEPS, finish)
        nc.all_engine_barrier()


BETWEEN_STEPS = 151
FINISH_STEPS = 138

CHUNK = 1024
SLOTS = 8
HALF = PAIRS // 2
N_CHUNKS = TILES * SLOTS


def pipeline(engine, slot, lag):
    for k in range(SLOTS):
        slot(0, k)
    with engine.Fori(1, TILES) as tile:
        for k in range(SLOTS):
            slot(tile, k)
    for k in range(lag):
        slot(TILES, k)


def lagged(tile, k, lag):
    k -= lag
    if k < 0:
        tile, k = tile - 1, k + SLOTS
    if isinstance(tile, int) and not 0 <= tile < TILES:
        return None
    return tile, k


def filter_stage(nc, ctx, own, PS, apart, adj_pairs, adj_sq, rfT, yT, W1pad, W2T, cols, half_col):
    V, A, PE, GP, SP = nc.vector, nc.scalar, nc.tensor, nc.gpsimd, nc.sync

    def sem(name):
        return own.enter_context(nc.semaphore(name))

    def sb(name, shape):
        return own.enter_context(nc.sbuf_tensor(name, shape, F32))

    E = [sb(f"f_adj{h}", [P, HALF]) for h in range(2)]
    G = [sb(f"f_gauss{h}", [P, HALF]) for h in range(2)]
    A2 = [[sb(f"f_sq{h}{b}", [P, HALF]) for b in range(2)] for h in range(2)]
    EX = [sb(f"f_ex{n}", [P, CHUNK]) for n in range(2)]
    Hs = [sb(f"f_h{n}", [P, CHUNK]) for n in range(2)]
    GATE = [sb(f"f_gate{n}", [P, CHUNK]) for n in range(2)]
    PR = [sb(f"f_prod{n}", [P, CHUNK]) for n in range(2)]
    PIECE = BANK

    def pre(n):
        return PS[:, 2 * n:2 * n + 2, :].rearrange("p b n -> p (b n)")

    def post(n):
        return PS[:, 4 + 2 * n:6 + 2 * n, :].rearrange("p b n -> p (b n)")

    s_adj = [sem(f"s_adj{h}") for h in range(2)]
    s_sq = [[sem(f"s_sq{h}{b}") for b in range(2)] for h in range(2)]
    s_diff, s_gauss = sem("s_diff"), sem("s_gauss")
    s_pre, s_exp, s_cap, s_ln, s_ssp = sem("s_pre"), sem("s_exp"), sem("s_cap"), sem("s_ln"), sem("s_ssp")
    s_post, s_gate, s_prod, s_sum = sem("s_post"), sem("s_gate"), sem("s_prod"), sem("s_sum")

    def done(engine, s, tile, k, ahead):
        count = tile * SLOTS + (k + ahead)
        if isinstance(count, int) and count <= 0:
            return
        engine.wait_ge(s, count)

    def parts(k):
        return k // 4, (k // 2) % 2, k % 2

    def load_half(tile, h):
        done(SP, s_gauss, tile, 4 * h, -4)
        for b in range(2):
            row = adj_pairs[bass.ds(tile * 2 + b, 1), h * HALF:(h + 1) * HALF]
            SP.dma_start(E[h][b * NG:(b + 1) * NG, :], row.broadcast_to([NG, HALF])).then_inc(s_adj[h], 16)

    def load_squares(tile, h):
        for b in range(2):
            done(SP, s_gate, tile, 4 * h + 2 * b, -6)
            row = adj_sq[bass.ds(tile * 2 + b, 1), h * HALF:(h + 1) * HALF]
            SP.dma_start(A2[h][b][:], row.broadcast_to([P, HALF])).then_inc(s_sq[h][b], 16)

    for h in range(2):
        load_half(0, h)
        load_squares(0, h)
    with SP.Fori(1, TILES) as tile:
        for h in range(2):
            load_half(tile, h)
            load_squares(tile, h)

    def act_slot(tile, k):
        at = lagged(tile, k, 5)
        if at:
            t_, k_ = at
            done(A, s_cap, t_, k_, 1)
            A.activation(EX[k_ % 2][:], EX[k_ % 2][:], ACT.Ln, bias=half_col[:], scale=0.5).then_inc(s_ln, 1)
        at = lagged(tile, k, 4)
        if at:
            t_, k_ = at
            done(A, s_pre, t_, k_, 1)
            done(A, s_ssp, t_, k_, -1)
            A.activation(EX[k_ % 2][:], pre(k_ % 2), ACT.Exp, bias=cols["b1"][:]).then_inc(s_exp, 1)
        at = lagged(tile, k, 0)
        if at:
            h, r = k // 4, k % 4
            piece = slice(r * PIECE, (r + 1) * PIECE)
            if r == 0:
                A.wait_ge(s_adj[h], tile * 32 + 32)
                done(A, s_pre, tile, 4 * h, -4)
            A.activation(E[h][:, piece], E[h][:, piece], ACT.Square, bias=cols["off"][:]).then_inc(s_diff, 1)
            done(A, s_diff, tile, k, 1)
            A.activation(G[h][:, piece], E[h][:, piece], ACT.Exp, scale=COEFF).then_inc(s_gauss, 1)

    A.preload_act_table_set("natural_log_exp_and_others")
    pipeline(A, act_slot, 5)

    def pe_slot(tile, k):
        at = lagged(tile, k, 4)
        if at:
            t_, k_ = at
            h, b, c = parts(k_)
            done(PE, s_gauss, t_, 4 * h, 2 * c + 2)
            done(PE, s_ssp, t_, k_, -1)
            for n in range(2):
                last = PE.matmul(PS[:, 2 * (k_ % 2) + n, :], W1pad[:, b, :],
                                 G[h][:, c * CHUNK + n * BANK:c * CHUNK + (n + 1) * BANK], start=True, stop=True)
            last.then_inc(s_pre, 1)
        at = lagged(tile, k, 6)
        if at:
            t_, k_ = at
            done(PE, s_ssp, t_, k_, 1)
            done(PE, s_prod, t_, k_, -1)
            for n in range(2):
                last = PE.matmul(PS[:, 4 + 2 * (k_ % 2) + n, :], W2T[:],
                                 Hs[k_ % 2][:, n * BANK:(n + 1) * BANK], start=True, stop=True)
            last.then_inc(s_post, 1)

    pipeline(PE, pe_slot, 6)

    def i_major(ap):
        return ap.rearrange("p (i j) -> p i j", j=NODES)

    def gp_slot(tile, k):
        at = lagged(tile, k, 6)
        if at:
            t_, k_ = at
            h, b, c = parts(k_)
            GP.wait_ge(s_sq[h][b], t_ * 16 + 16)
            done(GP, s_prod, t_, k_, -1)
            GP.sem_inc(apart, 1)
            rf = rfT[:, bass.ds(t_ * P + b * NODES, NODES)].unsqueeze(1).broadcast_to([P, CHUNK // NODES, NODES])
            GP.tensor_tensor(i_major(GATE[k_ % 2][:]), rf, i_major(A2[h][b][:, c * CHUNK:(c + 1) * CHUNK]),
                             ALU.mult).then_inc(s_gate, 1)

    pipeline(GP, gp_slot, 6)

    def dve_slot(tile, k):
        at = lagged(tile, k, 5)
        if at:
            t_, k_ = at
            done(V, s_exp, t_, k_, 1)
            V.tensor_scalar(EX[k_ % 2][:], EX[k_ % 2][:], EXP_CAP, None, ALU.min).then_inc(s_cap, 1)
        at = lagged(tile, k, 7)
        if at:
            t_, k_ = at
            h, b, c = parts(k_)
            done(V, s_post, t_, k_, 1)
            done(V, s_gate, t_, k_, 1)
            done(V, s_sum, t_, k_, -1)
            V.scalar_tensor_tensor(PR[k_ % 2][:], post(k_ % 2), cols["b2"][:], GATE[k_ % 2][:],
                                   ALU.add, ALU.mult).then_inc(s_prod, 1)
            done(V, s_prod, t_, k_, 1)
            first = b * NODES + h * (NODES // 2) + c * (CHUNK // NODES)
            V.tensor_reduce(yT[:, bass.ds(t_ * P + first, CHUNK // NODES)], i_major(PR[k_ % 2][:]),
                            AX, ALU.add).then_inc(s_sum, 1)
        at = lagged(tile, k, 5)
        if at:
            t_, k_ = at
            done(V, s_ln, t_, k_, 1)
            done(V, s_post, t_, k_, -1)
            V.scalar_tensor_tensor(Hs[k_ % 2][:], pre(k_ % 2), cols["b1l"][:], EX[k_ % 2][:],
                                   ALU.add, ALU.max).then_inc(s_ssp, 1)

    pipeline(V, dve_slot, 7)


def attend_stage(nc, ctx, own, PS, apart, hw_d, hs_d, att_d, U, VT, w2sel, cols):
    V, A, PE, GP, SP = nc.vector, nc.scalar, nc.tensor, nc.gpsimd, nc.sync

    def sem(name):
        return own.enter_context(nc.semaphore(name))

    def sb(name, shape):
        return own.enter_context(nc.sbuf_tensor(name, shape, F32))

    Q = [sb(f"a_q{b}", [P, PAIRS]) for b in range(2)]
    QU = sb("a_qu", [P, PAIRS])
    ST = [sb(f"a_w{b}", [P, P]) for b in range(2)]
    SI = [sb(f"a_silu{n}", [P, CHUNK]) for n in range(2)]
    W2 = [sb(f"a_w2{b}", [P, 2, 32]) for b in range(2)]
    ATT = sb("a_att", [P, BANK])
    VS, US = sb("a_vs", [P, NODES]), sb("a_us", [P, NODES])
    Z = 7
    att_out = att_d.rearrange("(g m q i) j -> g q m (i j)", g=GROUPS, q=4, i=BANK // NODES)

    s_w = [sem(f"s_w{b}") for b in range(2)]
    s_ones, s_v, s_u, s_q = sem("s_ones"), sem("s_v"), sem("s_u"), sem("s_q")
    s_vs, s_us = sem("s_vs"), sem("s_us")
    s_sel, s_first, s_silu, s_dot = sem("s_sel"), sem("s_first"), sem("s_silu"), sem("s_dot")
    s_tanh, s_out = sem("s_tanh"), sem("s_out")
    SILU_0, DOT_0, TANH_0, OUT_0 = 2, 5, 1, 1
    A.nop().then_inc(s_silu, SILU_0)
    PE.nop().then_inc(s_dot, DOT_0)
    A.nop().then_inc(s_tanh, TANH_0)
    SP.nop().then_inc(s_out, OUT_0)

    def rows_of(b):
        return slice(b * NODES, (b + 1) * NODES)

    def before(engine, s, count):
        if not isinstance(count, int) or count > 0:
            engine.wait_ge(s, count)

    def first_and_rest(engine, body):
        body(0)
        with engine.Fori(1, TILES) as tile:
            body(tile)

    def sp_tile(tile):
        for b in range(2):
            before(SP, s_first, (tile - 1) * 8 + (4 * b + 4))
            row = bass.ds(tile * P + b * NODES, NODES)
            SP.dma_start(ST[b][rows_of(b), :], hw_d[row, :]).then_inc(s_w[b], 16)
            SP.dma_start(ST[b][rows_of(1 - b), :], hs_d[row, :]).then_inc(s_w[b], 16)

    first_and_rest(SP, sp_tile)

    def by_pair(ap):
        return ap.rearrange("p (i j) -> p i j", j=NODES)

    square = [NODES, NODES, NODES]
    for b in range(2):
        GP.memset(Q[b][rows_of(1 - b), :], 1.0).then_inc(s_ones, 1)
    GP.wait_ge(s_ones, 2)
    for b in range(2):
        o = by_pair(Q[b][rows_of(1 - b), :])
        GP.affine_select(out=o, in_=o, compare_op=ALU.is_equal, fill=0.0, base=0,
                         pattern=[[-1, NODES], [0, NODES]], channel_multiplier=1).then_inc(s_ones, 1)

    def gp_tile(tile):
        for b in range(2):
            r = rows_of(b)
            before(GP, s_v, (tile - 1) * 2 + (b + 1))
            before(GP, s_u, (tile - 1) * 2 + (b + 1))
            GP.sem_inc(apart, 1)
            GP.tensor_copy(VS[r, :], VT[r, bass.ds(tile, 1), :].rearrange("p o i -> p (o i)")).then_inc(s_vs, 1)
            GP.tensor_copy(US[r, :], U[r, bass.ds(tile, 1), :].rearrange("p o j -> p (o j)")).then_inc(s_us, 1)
            before(GP, s_first, (tile - 1) * 8 + (4 * b + 4))
            GP.wait_ge(s_vs, tile * 2 + (b + 1))
            GP.sem_inc(apart, 1)
            GP.affine_select(out=by_pair(Q[b][r, :]), in_=VS[r, :].unsqueeze(2).broadcast_to(square),
                             compare_op=ALU.is_equal, fill=0.0, base=0,
                             pattern=[[0, NODES], [-1, NODES]], channel_multiplier=1).then_inc(s_v, 1)
            before(GP, s_q, (tile - 1) * 2 + (b + 1))
            GP.wait_ge(s_us, tile * 2 + (b + 1))
            GP.sem_inc(apart, 1)
            GP.affine_select(out=by_pair(QU[r, :]), in_=US[r, :].unsqueeze(1).broadcast_to(square),
                             compare_op=ALU.is_equal, fill=0.0, base=0,
                             pattern=[[-1, NODES], [0, NODES]], channel_multiplier=1).then_inc(s_u, 1)

    first_and_rest(GP, gp_tile)

    with V.Fori(0, GROUPS) as g:
        with V.Fori(0, GT) as tl:
            for b in range(2):
                r = rows_of(b)
                graphs = g * (2 * GT) + tl * 2 + (b + 1)
                V.wait_ge(s_v, graphs)
                V.wait_ge(s_u, graphs)
                V.tensor_tensor(Q[b][r, :], Q[b][r, :], QU[r, :], ALU.add).then_inc(s_q, 1)
                V.wait_ge(s_dot, g * (8 * GT) + tl * 8 + (4 * b + 4 - 8 + DOT_0))
                V.sem_inc(apart, 1)
                for c in range(2):
                    last = V.tensor_copy(W2[b][:, c, :], w2sel[:, bass.ds(32 - 2 * b - c - tl * 4, 32)])
                last.then_inc(s_sel, 1)

    def pe_slot(g, tl, k):
        n = g * (8 * GT) + (tl * 8 + k)
        if not isinstance(tl, int) or tl < GT:
            b, c = k // 4, k % 4
            if c == 0:
                PE.wait_ge(s_q, g * (2 * GT) + (tl * 2 + (b + 1)))
                PE.wait_ge(s_w[b], g * (32 * GT) + (tl * 32 + 32))
            PE.wait_ge(s_silu, n + (-1 + SILU_0))
            for m in range(2):
                last = PE.matmul(PS[:, 2 * (k % 2) + m, :], ST[b][:],
                                 Q[b][:, c * CHUNK + m * BANK:c * CHUNK + (m + 1) * BANK], start=True, stop=True)
            last.then_inc(s_first, 1)
        if isinstance(tl, int) and tl == 0 and k == 0:
            return
        tl, k = (tl, k - 1) if k else (tl - 1, 7)
        b, c = k // 4, k % 4
        head = isinstance(tl, int) and tl == 0 and k < 2
        if head and k == 0:
            PE.wait_ge(s_tanh, g + TANH_0)
        if c == 0:
            PE.wait_ge(s_sel, g * (2 * GT) + (tl * 2 + (b + 1)))
        PE.wait_ge(s_silu, n + (0 + SILU_0))
        for m in range(2):
            q = (2 * c + m) % 4
            last = PE.matmul(PS[32 * q:32 * q + 32, Z, :], W2[b][:, (2 * c + m) // 4, :],
                             SI[k % 2][:, m * BANK:(m + 1) * BANK], start=head, stop=True, skip_group_check=True)
        last.then_inc(s_dot, 1)

    PE.wait_ge(s_ones, 4)
    with PE.Fori(0, GROUPS) as g:
        for k in range(8):
            pe_slot(g, 0, k)
        with PE.Fori(1, GT) as tl:
            for k in range(8):
                pe_slot(g, tl, k)
        pe_slot(g, GT, 0)

    with A.Fori(0, GROUPS) as g:
        with A.Fori(0, GT) as tl:
            for k in range(8):
                n = g * (8 * GT) + tl * 8 + k
                A.wait_ge(s_first, n + 1)
                A.wait_ge(s_dot, n + (-1 + DOT_0))
                pre = PS[:, 2 * (k % 2):2 * (k % 2) + 2, :].rearrange("p b n -> p (b n)")
                A.activation(SI[k % 2][:], pre, ACT.Silu, bias=cols["att_b1"][:]).then_inc(s_silu, 1)
        A.wait_ge(s_dot, g * (8 * GT) + (8 * GT + DOT_0))
        A.wait_ge(s_out, g * 64 + OUT_0)
        A.activation(ATT[:], PS[:, Z, :], ACT.Tanh, scale=0.5, bias=cols["att_b2"][:]).then_inc(s_tanh, 1)
        A.wait_ge(s_tanh, g + (1 + TANH_0))
        for q in range(4):
            A.dma_start(att_out[bass.ds(g, 1), q, :, :].rearrange("o m n -> (o m) n"),
                        ATT[32 * q:32 * q + 32, :]).then_inc(s_out, 16)
    SP.wait_ge(s_out, GROUPS * 64 + OUT_0)


def kernel(**inputs):
    import numpy as _np
    import concourse.bacc as _bacc
    from concourse import mybir as _mybir
    from concourse.bass_utils import run_bass_kernel_spmd as _run

    turned = {"adj": "adjT", "L0_gnn_W1": "W1T", "L0_gnn_W2": "W2T", "L0_gnn_Wa": "WaT", "L0_gnn_Wd1": "Wd1T",
              "L0_gnn_Wd2": "Wd2T", "L1_gnn_W": "WT", "L1_gnn_att_w1": "WattT", "L1_gnn_mlp_w1": "Wm1T",
              "L1_gnn_mlp_w2": "Wm2T"}
    straight = ["x", "adj", "L0_gnn_b1", "L0_gnn_b2", "L0_gnn_bd1", "L0_gnn_bd2", "L1_gnn_b_lin",
                "L1_gnn_att_b1", "L1_gnn_att_w2", "L1_gnn_att_b2", "L1_gnn_mlp_b1", "L1_gnn_mlp_b2",
                "L2_gnn_W", "L2_gnn_b", "L3_gnn_W_msg", "L3_gnn_W_upd"]
    arrays = {n: _np.ascontiguousarray(inputs[n]) for n in straight}
    for n, name in turned.items():
        arrays[name] = _np.ascontiguousarray(_np.swapaxes(_np.asarray(inputs[n]), -1, -2))
    nc = _bacc.Bacc("TRN2", target_bir_lowering=False, num_devices=1)
    t = {n: nc.dram_tensor("in_" + n, a.shape, _mybir.dt.from_np(a.dtype), kind="ExternalInput").ap()
         for n, a in arrays.items()}
    out = nc.dram_tensor("out_x", arrays["x"].shape, _mybir.dt.float32, kind="ExternalOutput").ap()
    build(nc, t, out)
    r = _run(nc, [{"in_" + n: a for n, a in arrays.items()}], core_ids=[0])
    return r.results[0]["out_x"]
```

```python
from contextlib import ExitStack

import concourse.bass as bass
import numpy as np
from concourse import mybir

F32 = mybir.dt.float32
I32 = mybir.dt.int32
ALU = mybir.AluOpType
ACT = mybir.ActivationFunctionType
AX = mybir.AxisListType.X

P = 128
GRAPHS, NODES = 128, 64
NG = 64
CUTOFF = 5.0
TILES = GRAPHS // 2
PAIRS = NODES * NODES
BANK = 512
GT = 8
GROUPS = TILES // GT
GB = GT * P // BANK
CHAINS = 8 // (2 * GB)
LN2 = float(np.log(2.0))
OFFSETS = np.linspace(0.0, CUTOFF, NG, dtype=np.float32)
COEFF = float(np.float32(-0.5) / ((OFFSETS[1] - OFFSETS[0]) * (OFFSETS[1] - OFFSETS[0])))
EXP_CAP = 2.0 ** 60
MIN_NORM = 1e-15
MAX_NORM = 1.0 - 0.004
ONE_LESS = 1.0 - 1e-7
SMALL_SQ = 1.0 / 64
LN_EPS = 1e-5


class Chain:

    def __init__(self, nc, sem, name, apart):
        self.nc, self.sem, self.done, self.apart = nc, sem(name), 0, apart
        self.signals = {"load": sem(name + "_load"), "store": sem(name + "_store")}
        self.signalled = {"load": 0, "store": 0}
        self.steps = None

    def step(self, engine, emit):
        if self.steps is not None:
            self.steps.append((engine, emit))
            return
        if self.done:
            engine.wait_ge(self.sem, self.done)
        emit().then_inc(self.sem, 1)
        self.done += 1

    def transfer(self, kind, pairs, wait=True):
        signal, sp = self.signals[kind], self.nc.sync
        self.signalled[kind] += 16 * len(pairs)
        upto = self.signalled[kind]

        def go():
            for dst, src in pairs:
                sp.dma_start(dst, src).then_inc(signal, 16)
            if wait:
                sp.wait_ge(signal, self.total(kind, upto))
                sp.sem_inc(self.apart, 1)
            return sp.nop()
        self.step(sp, go)

    def through(self, kind):
        signal, sp, upto = self.signals[kind], self.nc.sync, self.signalled[kind]

        def go():
            sp.wait_ge(signal, self.total(kind, upto))
            sp.sem_inc(self.apart, 1)
            return sp.nop()
        self.step(sp, go)

    def total(self, kind, upto):
        if self.steps is None:
            return upto
        return self.turn * (self.signalled[kind] - self.before[kind]) + upto


def loop_together(nc, turns, chains, body):
    with nc.Fori(0, turns) as turn:
        for n, c in enumerate(chains):
            c.turn, c.steps, c.before = turn, [], dict(c.signalled)
            body(turn, n)
        per = len(chains[0].steps)
        for k in range(per):
            for c in chains:
                engine, emit = c.steps[k]
                engine.wait_ge(c.sem, turn * per + (c.done + k))
                if engine is nc.sync:
                    engine.sem_inc(c.apart, 1)
                emit().then_inc(c.sem, 1)
    for c in chains:
        c.done += turns * per
        c.steps = None
        for kind in c.signalled:
            c.signalled[kind] = c.before[kind] + turns * (c.signalled[kind] - c.before[kind])


def build(nc, t, out):
    V, A, PE, GP, SP = nc.vector, nc.scalar, nc.tensor, nc.gpsimd, nc.sync
    ctx = ExitStack()
    with ctx:
        def sem(name):
            return ctx.enter_context(nc.semaphore(name))

        def sb(name, shape, dt=F32, where=ctx):
            return where.enter_context(nc.sbuf_tensor(name, shape, dt))

        def dram(name, shape):
            return nc.dram_tensor(name, shape, F32, kind="Internal").ap()

        PS = ctx.enter_context(nc.psum_tensor("PS", [P, 8, BANK], F32))

        def tiles(ap):
            return ap.rearrange("(t p) d -> p t d", p=P)

        x_in = tiles(t["x"].rearrange("b n d -> (b n) d"))
        x_out = tiles(out.rearrange("b n d -> (b n) d"))
        adj_pairs = t["adj"].rearrange("b i j -> b (i j)")
        adj_rows = tiles(t["adj"].rearrange("b i j -> (b i) j"))
        adjT_rows = tiles(t["adjT"].rearrange("b j i -> (b j) i"))
        adj_sq = dram("adj_sq", [GRAPHS, PAIRS])
        x1_d = dram("x1_d", [GRAPHS * NODES, P])
        h_d = dram("h_d", [GRAPHS * NODES, P])
        hw_d = dram("hw_d", [GRAPHS * NODES, P])
        hs_d = dram("hs_d", [GRAPHS * NODES, P])
        att_d = dram("att_d", [GRAPHS * NODES, NODES])

        apart = sem("apart")
        chains = [Chain(nc, sem, f"chain_{n}", apart) for n in range(CHAINS)]
        cur = [chains[0], 0]

        def v(emit): cur[0].step(V, emit)
        def a(emit): cur[0].step(A, emit)
        def pe(emit): cur[0].step(PE, emit)
        def gp(emit): cur[0].step(GP, emit)

        def together(body):
            def one(turn, n):
                cur[0], cur[1] = chains[n], n
                body(turn * CHAINS + n, n)
            loop_together(nc, GROUPS // CHAINS, chains, one)
            cur[0], cur[1] = chains[0], 0

        def load(pairs): cur[0].transfer("load", pairs)
        def store(pairs, wait=False): cur[0].transfer("store", pairs, wait)
        def stored(): cur[0].through("store")

        def const(name, shape):
            return sb(name, shape)

        W = {n: const("w_" + n, [P, P]) for n in
             ("WaT", "W2T", "Wd1T", "Wd2T", "WT", "Wm1LT", "Wm1RT", "Wm2T", "Wg", "Wmsg_s", "Wmsg_r", "Wub", "WsT", "WrT")}
        WrlT = const("WrlT", [P, 2 * P])
        W3 = const("W3", [P, 3 * P])
        W1pad = const("W1pad", [P, 2, P])
        w2sel = const("w2sel", [P, 64])
        cols = {n: const("c_" + n, [P, 1]) for n in
                ("b1", "b1l", "b2", "bd1", "bd1l", "att_b1", "mlp_b1", "att_w2", "att_b2", "off", "hb2")}
        rows = {n: const("r_" + n, [P, P]) for n in ("bd2", "hb", "mlp_b2", "L2_b")}
        ident = const("ident", [P, P])
        ones = const("ones", [P, NODES])
        big = sb("big", [P, TILES * P])
        rfT = big
        x2_all = const("x2_all", [P, TILES])
        cs_all = const("cs_all", [P, TILES])
        smalls = [const(f"small{n}", [P, 30, GT]) for n in range(CHAINS)]
        tmpc = const("tmpc", [P, 8])
        off_i = sb("off_i", [P, 1], I32)

        gp(lambda: GP.memset(ident[:], 0.0))
        gp(lambda: GP.affine_select(out=ident[:], in_=ident[:], compare_op=ALU.not_equal, fill=1.0,
                                    base=0, pattern=[[-1, P]], channel_multiplier=1))
        gp(lambda: GP.memset(ones[:], 1.0))
        gp(lambda: GP.memset(W1pad[:], 0.0))
        gp(lambda: GP.memset(w2sel[:], 0.0))
        gp(lambda: GP.iota(off_i[0:NG, :], [[0, 1]], base=0, channel_multiplier=1))
        gp(lambda: GP.iota(off_i[NG:P, :], [[0, 1]], base=0, channel_multiplier=1))

        def column(ap):
            return ap.rearrange("(p o) -> p o", o=1)

        def across(ap):
            return ap.rearrange("(o n) -> o n", o=1).broadcast_to([P, ap.shape[0]])

        load([
            (W["WaT"][:], t["WaT"]), (W["W2T"][:], t["W2T"]), (W["Wd1T"][:], t["Wd1T"]),
            (W["Wd2T"][:], t["Wd2T"]), (W["WT"][:], t["WT"]), (W["Wm2T"][:], t["Wm2T"]),
            (W["Wm1LT"][:], t["Wm1T"][0:P, :]), (W["Wm1RT"][:], t["Wm1T"][P:2 * P, :]),
            (W["Wg"][:], t["L2_gnn_W"]),
            (W["Wmsg_s"][:], t["L3_gnn_W_msg"][0:P, :]), (W["Wmsg_r"][:], t["L3_gnn_W_msg"][P:2 * P, :]),
            (W["Wub"][:], t["L3_gnn_W_upd"][P:2 * P, :]), (W3[:, P:2 * P], t["L3_gnn_W_upd"][0:P, :]),
            (WrlT[:, 0:P], t["WattT"][P:2 * P, :]), (WrlT[:, P:2 * P], t["WattT"][0:P, :]),
            (W1pad[0:NG, 0, :], t["W1T"]), (W1pad[NG:P, 1, :], t["W1T"]),
            (cols["b1"][:], column(t["L0_gnn_b1"])), (cols["b2"][:], column(t["L0_gnn_b2"])),
            (cols["bd1"][:], column(t["L0_gnn_bd1"])), (cols["att_b1"][:], column(t["L1_gnn_att_b1"])),
            (cols["mlp_b1"][:], column(t["L1_gnn_mlp_b1"])),
            (cols["att_w2"][:], t["L1_gnn_att_w2"].rearrange("o p -> p o")),
            (cols["att_b2"][:], across(t["L1_gnn_att_b2"])),
            (rows["bd2"][:], across(t["L0_gnn_bd2"])), (rows["hb"][:], across(t["L1_gnn_b_lin"])),
            (rows["mlp_b2"][:], across(t["L1_gnn_mlp_b2"])), (rows["L2_b"][:], across(t["L2_gnn_b"])),
        ])
        v(lambda: V.tensor_copy(w2sel[:, 32:33], cols["att_w2"][:]))
        v(lambda: V.tensor_copy(cols["off"][:], off_i[:]))
        v(lambda: V.tensor_scalar(cols["off"][:], cols["off"][:], -CUTOFF, 1.0 / (NG - 1), ALU.mult, ALU.mult))
        v(lambda: V.tensor_scalar(cols["b1l"][:], cols["b1"][:], -LN2, None, ALU.add))
        v(lambda: V.tensor_scalar(cols["bd1l"][:], cols["bd1"][:], -LN2, None, ALU.add))
        v(lambda: V.tensor_scalar(cols["att_b2"][:], cols["att_b2"][:], 0.5, None, ALU.mult))

        pe(lambda: PE.transpose(PS[:, 0, 0:P], W["Wmsg_s"][:], ident[:]))
        pe(lambda: PE.transpose(PS[:, 1, 0:P], W["Wmsg_r"][:], ident[:]))
        v(lambda: V.tensor_copy(W["WsT"][:], PS[:, 0, 0:P]))
        v(lambda: V.tensor_copy(W["WrT"][:], PS[:, 1, 0:P]))
        pe(lambda: PE.matmul(PS[:, 0, 0:P], W["WsT"][:], W["Wub"][:], start=True, stop=True))
        pe(lambda: PE.matmul(PS[:, 1, 0:P], W["WrT"][:], W["Wub"][:], start=True, stop=True))
        v(lambda: V.tensor_copy(W3[:, 0:P], PS[:, 0, 0:P]))
        v(lambda: V.tensor_copy(W3[:, 2 * P:3 * P], PS[:, 1, 0:P]))

        def ts(o, i, s1, op0, s2=None, op1=None):
            if op1 is None:
                v(lambda: V.tensor_scalar(o, i, s1, None, op0))
            else:
                v(lambda: V.tensor_scalar(o, i, s1, s2, op0, op1))

        def tt(o, x, y, op):
            v(lambda: V.tensor_tensor(o, x, y, op))

        def stt(o, x, s, y, op0, op1):
            v(lambda: V.scalar_tensor_tensor(o, x, s, y, op0, op1))

        def recip(o, i):
            v(lambda: V.reciprocal(o, i))

        def act(o, i, f, scale=1.0, bias=0.0):
            a(lambda: A.activation(o, i, f, bias=bias, scale=scale))

        def rsum(o, i):
            v(lambda: V.tensor_reduce(o, i, AX, ALU.add))

        def series(o, q):
            ts(o, q, 1.0 / 11, ALU.mult)
            for d in (9, 7, 5, 3):
                stt(o, o, 1.0 / d, q, ALU.add, ALU.mult)
            ts(o, o, 1.0, ALU.add)

        def artanh_over(o, q, z, ratio, m, w):
            act(w, ratio, ACT.Ln)
            ts(m, z, 0.1, ALU.max)
            recip(m, m)
            stt(w, w, 0.5, m, ALU.mult, ALU.mult)
            series(o, q)
            tt(w, w, o, ALU.subtract)
            ts(m, q, SMALL_SQ, ALU.is_ge)
            tt(w, w, m, ALU.mult)
            tt(o, o, w, ALU.add)

        def artanh(o, z, q, ratio, m, w):
            ts(m, z, -1.0, ALU.mult, 1.0, ALU.add)
            recip(m, m)
            stt(ratio, z, 1.0, m, ALU.add, ALU.mult)
            tt(q, z, z, ALU.mult)
            artanh_over(o, q, z, ratio, m, w)
            tt(o, o, z, ALU.mult)

        with ExitStack() as c0:
            sq = sb("sq0", [P, P], where=c0)
            tt(sq[:], rows["hb"][:], rows["hb"][:], ALU.mult)
            rsum(tmpc[:, 0:1], sq[:])
            act(tmpc[:, 1:2], tmpc[:, 0:1], ACT.Sqrt)
            ts(tmpc[:, 1:2], tmpc[:, 1:2], MIN_NORM, ALU.max)
            recip(tmpc[:, 2:3], tmpc[:, 1:2])
            act(tmpc[:, 3:4], tmpc[:, 1:2], ACT.Tanh)
            ts(tmpc[:, 3:4], tmpc[:, 3:4], MAX_NORM, ALU.min)
            tt(tmpc[:, 3:4], tmpc[:, 3:4], tmpc[:, 2:3], ALU.mult)
            ts(rows["hb"][:], rows["hb"][:], tmpc[:, 3:4], ALU.mult)
            tt(sq[:], rows["hb"][:], rows["hb"][:], ALU.mult)
            rsum(cols["hb2"][:], sq[:])

            ad = sb("ad", [P, PAIRS], where=c0)
            load([(ad[:], adj_pairs)])
            tt(ad[:], ad[:], ad[:], ALU.mult)
            store([(adj_sq, ad[:])], wait=True)

        def bc(col):
            return col.unsqueeze(2).broadcast_to([P, GT, P])

        def brow(row):
            return row[:].unsqueeze(1).broadcast_to([P, GT, P])

        def flat(buf):
            return buf[:].rearrange("p t d -> p (t d)")

        def S(n):
            return smalls[cur[1]][:, n, :]

        def place(n, width=P):
            first = (2 * cur[1] + n) * GB
            return PS[:, first:first + GB * width // P, :].rearrange("p b (t d) -> p (b t) d", d=width)

        def columns(n):
            return place(n).rearrange("p t d -> p (t d)")

        def norm_relu(X, XC, SQ, H, extra=None):
            rsum(S(0), X[:])
            ts(S(0), S(0), 1.0 / P, ALU.mult)
            tt(XC[:], X[:], bc(S(0)), ALU.subtract)
            squares(S(1), XC, SQ)
            ts(S(1), S(1), 1.0 / P, ALU.mult, LN_EPS, ALU.add)
            act(S(1), S(1), ACT.Sqrt)
            recip(S(1), S(1))
            if extra is not None:
                tt(S(1), S(1), extra, ALU.mult)
            stt(H[:], XC[:], 0.0, bc(S(1)), ALU.max, ALU.mult)

        def turn_tiles(SRC, n, DST):
            to = place(n)

            def go():
                for k in range(GT):
                    last = PE.transpose(to[:, k, :], SRC[:, k, :], ident[:])
                return last
            pe(go)
            act(flat(DST), columns(n), ACT.Copy)

        def wide(at, parts):
            to = columns(at)

            def go():
                for c in range(GB):
                    for n, (w, cols_of) in enumerate(parts):
                        last = PE.matmul(to[:, c * BANK:(c + 1) * BANK], w, cols_of(c),
                                         start=n == 0, stop=n == len(parts) - 1)
                return last
            pe(go)

        def half(buf):
            return lambda c: flat(buf)[:, c * BANK:(c + 1) * BANK]

        def per_tile(n, lhs, rhs, width=P):
            region = place(n, width)

            def go():
                for k in range(GT):
                    last = PE.matmul(region[:, k, :], lhs(k), rhs(k), start=True, stop=True)
                return last
            pe(go)
            return region

        def ssp(o, i, bias, bias_l):
            act(o, i, ACT.Exp, bias=bias)
            ts(o, o, EXP_CAP, ALU.min)
            act(o, o, ACT.Ln, scale=0.5, bias=half_col[:])
            stt(o, i, bias_l, o, ALU.add, ALU.max)

        half_col = const("half_col", [P, 1])
        v(lambda: V.memset(half_col[:], 0.5))

        def squares(o, X, SQ):
            act(SQ[:], X[:], ACT.Square)
            rsum(o, SQ[:])

        def gtt(o, x, y, op):
            gp(lambda: GP.tensor_tensor(o, x, y, op))

        def buffers(names, tag, where, width=P):
            return [[sb(f"{n}{tag}{c}", [P, GT, width], where=where) for n in names] for c in range(CHAINS)]

        with ExitStack() as c1:
            bufs = buffers(("X", "XC", "SQ", "H", "HT"), "1", c1)

            def prepare(g, n):
                X, XC, SQ, H, HT = bufs[n]
                load([(X[:], x_in[:, bass.ds(g * GT, GT), :])])
                norm_relu(X, XC, SQ, H)
                turn_tiles(H, 0, HT)
                wide(1, [(W["WaT"][:], half(HT))])
                act(rfT[:, bass.ds(g * (GT * P), GT * P)], columns(1), ACT.Copy)

            for c in chains[1:]:
                c.step(SP, lambda: SP.nop())
            together(prepare)
        nc.all_engine_barrier()

        yT = sb("yT", [P, TILES * P])
        with ExitStack() as c2:
            filter_stage(nc, c2, PS, apart, adj_pairs, adj_sq, rfT, yT, W1pad, W["W2T"], cols, half_col)
        nc.all_engine_barrier()

        U = big[:, 0:TILES * NODES].rearrange("p (t j) -> p t j", j=NODES)
        VT = big[:, TILES * NODES:].rearrange("p (t j) -> p t j", j=NODES)
        VP = sb("VP", [P, TILES, NODES])
        with ExitStack() as c3:
            bufs = buffers(("X", "XC", "SQ", "H", "HT", "MX"), "3", c3)
            pair_bufs = buffers(("y2", "a1", "den", "n1", "q", "z", "m", "w", "T", "oy"), "q", c3, NODES)

            def between(g, n):
                X, XC, SQ, H, HT, MX = bufs[n]
                y2, a1, den, n1, q, z, m, w, T, oy = (x[:] for x in pair_bufs[n])
                nodes = bass.ds(g * GT, GT)
                load([(X[:], x_in[:, nodes, :])])
                to = columns(0)
                pe(lambda: [PE.matmul(to[:, c * BANK:(c + 1) * BANK], W["Wd1T"][:],
                                      yT[:, bass.ds(g * (GT * P) + c * BANK, BANK)],
                                      start=True, stop=True) for c in range(GB)][-1])
                ssp(flat(HT), columns(0), cols["bd1"][:], cols["bd1l"][:])
                y3 = per_tile(1, lambda k: HT[:, k, :], lambda k: W["Wd2T"][:])
                tt(X[:], y3, X[:], ALU.add)
                gtt(X[:], X[:], brow(rows["bd2"]), ALU.add)
                store([(tiles(x1_d)[:, nodes, :], X[:])])
                norm_relu(X, XC, SQ, H)
                turn_tiles(H, 0, HT)
                squares(S(2), H, SQ)
                mx = per_tile(1, lambda k: HT[:, k, :], lambda k: W["WT"][:])
                act(MX[:], mx, ACT.Copy)
                squares(S(3), MX, SQ)
                gtt(SQ[:], MX[:], brow(rows["hb"]), ALU.mult)
                rsum(S(4), SQ[:])
                act(S(5), S(2), ACT.Sqrt)
                act(S(6), S(3), ACT.Sqrt)
                ts(S(5), S(5), MIN_NORM, ALU.max)
                ts(S(6), S(6), MIN_NORM, ALU.max)
                ts(S(7), S(5), ONE_LESS, ALU.min)
                artanh(S(8), S(7), S(9), S(10), S(11), S(12))
                recip(S(13), S(5))
                recip(S(14), S(6))
                tt(S(8), S(8), S(13), ALU.mult)
                tt(S(8), S(8), S(6), ALU.mult)
                act(S(8), S(8), ACT.Tanh)
                ts(S(8), S(8), MAX_NORM, ALU.min)
                tt(S(8), S(8), S(14), ALU.mult)
                tt(S(15), S(8), S(8), ALU.mult)
                tt(S(15), S(15), S(3), ALU.mult)
                tt(S(16), S(8), S(4), ALU.mult)
                ts(S(16), S(16), 2.0, ALU.mult, 1.0, ALU.add)
                stt(S(17), S(15), cols["hb2"][:], S(16), ALU.mult, ALU.add)
                ts(S(17), S(17), MIN_NORM, ALU.max)
                recip(S(17), S(17))
                stt(S(16), S(16), cols["hb2"][:], S(8), ALU.add, ALU.mult)
                tt(S(16), S(16), S(17), ALU.mult)
                ts(S(15), S(15), -1.0, ALU.mult, 1.0, ALU.add)
                tt(S(15), S(15), S(17), ALU.mult)
                tt(H[:], MX[:], bc(S(16)), ALU.mult)
                gtt(SQ[:], brow(rows["hb"]), bc(S(15)), ALU.mult)
                tt(H[:], H[:], SQ[:], ALU.add)
                squares(S(18), H, SQ)
                act(S(19), S(18), ACT.Sqrt)
                ts(S(19), S(19), MIN_NORM, ALU.max)
                recip(S(19), S(19))
                ts(S(19), S(19), MAX_NORM, ALU.mult, 1.0, ALU.min)
                tt(H[:], H[:], bc(S(19)), ALU.mult)
                squares(S(20), H, SQ)
                x2, x2_1 = S(20), S(21)
                v(lambda: V.tensor_copy(x2_all[:, nodes], x2))
                ts(x2_1, x2, -1.0, ALU.mult, 1.0, ALU.add)
                ts(S(22), x2, -2.0, ALU.mult, 1.0, ALU.add)
                tt(S(23), S(22), x2, ALU.add)
                tt(S(23), x2_1, S(23), ALU.subtract)
                tt(S(24), x2, x2, ALU.mult)
                tt(S(24), S(24), S(22), ALU.add)
                recip(S(24), S(24))
                tt(S(23), S(23), S(24), ALU.mult)
                tt(S(24), S(23), S(23), ALU.mult)
                tt(S(24), S(24), x2, ALU.mult)
                series(S(25), S(24))
                tt(S(25), S(25), S(23), ALU.mult)
                tt(S(25), S(25), x2_1, ALU.mult)
                cs = S(25)
                v(lambda: V.tensor_copy(cs_all[:, nodes], cs))
                turn_tiles(H, 0, HT)
                r = per_tile(0, lambda k: HT[:, k, :], lambda k: WrlT[:], 2 * P)
                act(XC[:], r[:, :, 0:P], ACT.Copy)
                tt(SQ[:], r[:, :, P:2 * P], bc(cs), ALU.mult)
                store([(tiles(h_d)[:, nodes, :], H[:]), (tiles(hw_d)[:, nodes, :], XC[:]),
                       (tiles(hs_d)[:, nodes, :], SQ[:])])
                act(MX[:], HT[:], ACT.Square)
                first = 2 * GB * cur[1]

                def dots():
                    for k in range(GT):
                        for b in range(2):
                            ri = slice(b * NODES, (b + 1) * NODES)
                            cj = slice(k * NODES, (k + 1) * NODES)
                            PE.matmul(PS[ri, first, cj], HT[:, k, ri], HT[:, k, ri], start=True, stop=True)
                            last = PE.matmul(PS[ri, first + 1, cj], ones[:], MX[:, k, ri], start=True, stop=True)
                    return last
                pe(dots)
                G = PS[:, first, 0:GT * NODES].rearrange("p (t j) -> p t j", j=NODES)
                Y2 = PS[:, first + 1, 0:GT * NODES].rearrange("p (t j) -> p t j", j=NODES)

                def of_i(col):
                    return col.unsqueeze(2).broadcast_to([P, GT, NODES])
                act(y2, Y2, ACT.Copy)
                ts(a1, G, -2.0, ALU.mult, 1.0, ALU.add)
                gtt(den, y2, of_i(x2), ALU.mult)
                ts(oy, y2, -1.0, ALU.mult, 1.0, ALU.add)
                tt(den, den, a1, ALU.add)
                ts(den, den, MIN_NORM, ALU.max)
                gtt(m, oy, of_i(x2_1), ALU.mult)
                stt(q, G, -2.0, y2, ALU.mult, ALU.add)
                tt(q, q, of_i(x2), ALU.add)
                tt(T, den, m, ALU.mult)
                recip(T, T)
                gtt(n1, a1, y2, ALU.add)
                tt(a1, T, m, ALU.mult)
                stt(q, q, 0.0, a1, ALU.max, ALU.mult)
                act(z, q, ACT.Sqrt)
                tt(m, T, den, ALU.mult)
                gtt(m, m, den, ALU.mult)
                stt(w, z, 1.0, m, ALU.add, ALU.mult)
                stt(w, z, 1.0, w, ALU.add, ALU.mult)
                artanh_over(T, q, z, w, m, w)
                tt(T, T, a1, ALU.mult)
                act(m, oy, ACT.Square)
                tt(VT[:, nodes, :], m, T, ALU.mult)
                gtt(m, T, of_i(x2_1), ALU.mult)
                tt(VP[:, nodes, :], m, of_i(x2_1), ALU.mult)
                stt(U[:, nodes, :], m, -1.0, n1, ALU.mult, ALU.mult)
                stored()

            together(between)
        nc.all_engine_barrier()

        with ExitStack() as c4:
            attend_stage(nc, c4, PS, apart, hw_d, hs_d, att_d, U, VT, w2sel, cols)
        nc.all_engine_barrier()

        with ExitStack() as c5:
            bufs = buffers(("X", "XC", "SQ", "H", "ST", "UU", "AV", "AB", "ABT"), "5", c5)
            pair_bufs = buffers(("at", "am"), "p", c5, NODES)
            for c in range(CHAINS):
                for buf in bufs[c][-3:]:
                    v(lambda buf=buf: V.memset(buf[:], 0.0))
            nc.all_engine_barrier()

            def two_blocks(buf):
                return [(slice(0, NODES), buf[0:NODES, :, 0:NODES]), (slice(NODES, P), buf[NODES:P, :, NODES:P])]

            def finish(g, n):
                X, XC, SQ, H, ST, UU, AV, AB, ABT = bufs[n]
                at, am = pair_bufs[n]
                nodes = bass.ds(g * GT, GT)
                stored()
                load([(X[:], tiles(x1_d)[:, nodes, :]), (H[:], tiles(h_d)[:, nodes, :]),
                      (at[:], tiles(att_d)[:, nodes, :]), (am[:], adj_rows[:, nodes, :])]
                     + [(blk, adj_rows[r, nodes, :]) for r, blk in two_blocks(AB)]
                     + [(blk, adjT_rows[r, nodes, :]) for r, blk in two_blocks(ABT)])
                ts(at[:], at[:], 0.5, ALU.mult, 0.5, ALU.add)
                gtt(am[:], am[:], at[:], ALU.mult)
                tt(at[:], am[:], U[:, nodes, :], ALU.mult)
                rsum(S(0), at[:])
                for r, blk in two_blocks(AV):
                    tt(blk, am[r, :, :], VP[r, nodes, :], ALU.mult)
                small = smalls[cur[1]]
                v(lambda: [V.scalar_tensor_tensor(AV[:, k, :], ident[:], small[:, 0, k:k + 1], AV[:, k, :],
                                                  ALU.mult, ALU.add) for k in range(GT)][-1])
                turn_tiles(AV, 0, XC)
                sup = per_tile(1, lambda k: H[:, k, :], lambda k: XC[:, k, :])
                act(ST[:], sup, ACT.Copy)
                tt(UU[:], H[:], bc(cs_all[:, nodes]), ALU.mult)
                turn_tiles(UU, 0, SQ)
                wide(1, [(W["Wm1LT"][:], half(SQ)), (W["Wm1RT"][:], half(ST))])
                act(flat(ST), columns(1), ACT.Silu, bias=cols["mlp_b1"][:])
                gtt(UU[:], UU[:], brow(rows["mlp_b2"]), ALU.add)
                z2 = per_tile(0, lambda k: ST[:, k, :], lambda k: W["Wm2T"][:])
                tt(UU[:], z2, UU[:], ALU.add)
                squares(S(1), UU, SQ)
                gtt(SQ[:], H[:], UU[:], ALU.mult)
                rsum(S(2), SQ[:])
                x2 = S(3)
                v(lambda: V.tensor_copy(x2, x2_all[:, nodes]))
                ts(S(4), S(3), -1.0, ALU.mult, 1.0, ALU.add)
                act(S(5), S(1), ACT.Sqrt)
                ts(S(5), S(5), MIN_NORM, ALU.max)
                ts(S(6), S(4), MIN_NORM, ALU.max)
                recip(S(6), S(6))
                tt(S(6), S(6), S(5), ALU.mult)
                act(S(6), S(6), ACT.Tanh)
                recip(S(7), S(5))
                tt(S(6), S(6), S(7), ALU.mult)
                tt(S(8), S(6), S(6), ALU.mult)
                tt(S(8), S(8), S(1), ALU.mult)
                tt(S(9), S(6), S(2), ALU.mult)
                ts(S(9), S(9), 2.0, ALU.mult, 1.0, ALU.add)
                tt(S(10), S(8), S(3), ALU.mult)
                tt(S(10), S(10), S(9), ALU.add)
                ts(S(10), S(10), MIN_NORM, ALU.max)
                recip(S(10), S(10))
                tt(S(9), S(9), S(8), ALU.add)
                tt(S(9), S(9), S(10), ALU.mult)
                tt(S(4), S(4), S(6), ALU.mult)
                tt(S(4), S(4), S(10), ALU.mult)
                gtt(UU[:], UU[:], bc(S(4)), ALU.mult)
                tt(H[:], H[:], bc(S(9)), ALU.mult)
                tt(H[:], H[:], UU[:], ALU.add)
                squares(S(11), H, SQ)
                act(S(12), S(11), ACT.Sqrt)
                ts(S(13), S(12), MIN_NORM, ALU.max)
                recip(S(14), S(13))
                ts(S(14), S(14), MAX_NORM, ALU.mult, 1.0, ALU.min)
                tt(S(15), S(13), S(14), ALU.mult)
                ts(S(15), S(15), MIN_NORM, ALU.max)
                ts(S(16), S(15), ONE_LESS, ALU.min)
                artanh(S(17), S(16), S(18), S(19), S(20), S(21))
                recip(S(15), S(15))
                tt(S(17), S(17), S(15), ALU.mult)
                tt(S(17), S(17), S(14), ALU.mult)
                tt(H[:], H[:], bc(S(17)), ALU.mult)
                act(H[:], H[:], ACT.Silu)
                squares(S(22), H, SQ)
                act(S(23), S(22), ACT.Sqrt)
                ts(S(23), S(23), MIN_NORM, ALU.max)
                recip(S(24), S(23))
                act(S(23), S(23), ACT.Tanh)
                ts(S(23), S(23), MAX_NORM, ALU.min)
                tt(S(23), S(23), S(24), ALU.mult)
                tt(H[:], H[:], bc(S(23)), ALU.mult)
                tt(X[:], X[:], H[:], ALU.add)
                rsum(S(25), AB[:])
                ts(S(25), S(25), 1e-8, ALU.add)
                act(S(25), S(25), ACT.Sqrt)
                recip(S(25), S(25))
                norm_relu(X, XC, SQ, H, extra=S(25))
                sup = per_tile(0, lambda k: H[:, k, :], lambda k: ABT[:, k, :])
                act(ST[:], sup, ACT.Copy)
                y = per_tile(1, lambda k: ST[:, k, :], lambda k: W["Wg"][:])
                gtt(X[:], X[:], brow(rows["L2_b"]), ALU.add)
                tt(SQ[:], y, bc(S(25)), ALU.mult)
                tt(X[:], X[:], SQ[:], ALU.add)
                norm_relu(X, XC, SQ, H)
                turn_tiles(H, 0, UU)
                rsum(S(26), ABT[:])
                ts(S(27), S(26), 0.0, ALU.is_gt)
                ts(S(26), S(26), 1.0, ALU.max)
                recip(S(26), S(26))
                tt(S(26), S(26), S(27), ALU.mult)
                y = per_tile(0, lambda k: UU[:, k, :], lambda k: W3[:, 0:2 * P], 2 * P)
                act(XC[:], y[:, :, 0:P], ACT.Copy)
                tt(X[:], y[:, :, P:2 * P], X[:], ALU.add)
                y = per_tile(0, lambda k: UU[:, k, :], lambda k: W3[:, 2 * P:3 * P])
                tt(SQ[:], y, bc(S(27)), ALU.mult)
                gtt(X[:], X[:], SQ[:], ALU.add)
                y = per_tile(1, lambda k: AB[:, k, :], lambda k: XC[:, k, :])
                tt(SQ[:], y, bc(S(26)), ALU.mult)
                tt(X[:], X[:], SQ[:], ALU.add)
                store([(x_out[:, nodes, :], X[:])])

            together(finish)
            for c in chains:
                SP.wait_ge(c.signals["store"], c.signalled["store"])
        nc.all_engine_barrier()


CHUNK = 1024
SLOTS = 8
HALF = PAIRS // 2
N_CHUNKS = TILES * SLOTS


def pipeline(engine, slot, lag):
    for k in range(SLOTS):
        slot(0, k)
    with engine.Fori(1, TILES) as tile:
        for k in range(SLOTS):
            slot(tile, k)
    for k in range(lag):
        slot(TILES, k)


def lagged(tile, k, lag):
    k -= lag
    if k < 0:
        tile, k = tile - 1, k + SLOTS
    if isinstance(tile, int) and not 0 <= tile < TILES:
        return None
    return tile, k


def filter_stage(nc, own, PS, apart, adj_pairs, adj_sq, rfT, yT, W1pad, W2T, cols, half_col):
    V, A, PE, GP, SP = nc.vector, nc.scalar, nc.tensor, nc.gpsimd, nc.sync

    def sem(name):
        return own.enter_context(nc.semaphore(name))

    def sb(name, shape):
        return own.enter_context(nc.sbuf_tensor(name, shape, F32))

    E = [sb(f"f_adj{h}", [P, HALF]) for h in range(2)]
    G = [sb(f"f_gauss{h}", [P, HALF]) for h in range(2)]
    A2 = [[sb(f"f_sq{h}{b}", [P, HALF]) for b in range(2)] for h in range(2)]
    EX = [sb(f"f_ex{n}", [P, CHUNK]) for n in range(2)]
    Hs = [sb(f"f_h{n}", [P, CHUNK]) for n in range(2)]
    GATE = [sb(f"f_gate{n}", [P, CHUNK]) for n in range(2)]
    PR = [sb(f"f_prod{n}", [P, CHUNK]) for n in range(2)]
    HP = [sb(f"f_half{n}", [P, CHUNK // 2]) for n in range(2)]
    PIECE = BANK

    def pre(n):
        return PS[:, 2 * n:2 * n + 2, :].rearrange("p b n -> p (b n)")

    def post(n):
        return PS[:, 4 + 2 * n:6 + 2 * n, :].rearrange("p b n -> p (b n)")

    s_adj = [sem(f"s_adj{h}") for h in range(2)]
    s_sq = [[sem(f"s_sq{h}{b}") for b in range(2)] for h in range(2)]
    s_diff, s_gauss = sem("s_diff"), sem("s_gauss")
    s_pre, s_exp, s_cap, s_ln, s_ssp = sem("s_pre"), sem("s_exp"), sem("s_cap"), sem("s_ln"), sem("s_ssp")
    s_post, s_gate, s_prod, s_half, s_sum = sem("s_post"), sem("s_gate"), sem("s_prod"), sem("s_half"), sem("s_sum")

    def done(engine, s, tile, k, ahead):
        count = tile * SLOTS + (k + ahead)
        if isinstance(count, int) and count <= 0:
            return
        engine.wait_ge(s, count)

    def parts(k):
        return k // 4, (k // 2) % 2, k % 2

    def load_half(tile, h):
        done(SP, s_gauss, tile, 4 * h, -4)
        for b in range(2):
            row = adj_pairs[bass.ds(tile * 2 + b, 1), h * HALF:(h + 1) * HALF]
            SP.dma_start(E[h][b * NG:(b + 1) * NG, :], row.broadcast_to([NG, HALF])).then_inc(s_adj[h], 16)

    def load_squares(tile, h):
        for b in range(2):
            done(SP, s_gate, tile, 4 * h + 2 * b, -6)
            row = adj_sq[bass.ds(tile * 2 + b, 1), h * HALF:(h + 1) * HALF]
            SP.dma_start(A2[h][b][:], row.broadcast_to([P, HALF])).then_inc(s_sq[h][b], 16)

    for h in range(2):
        load_half(0, h)
        load_squares(0, h)
    with SP.Fori(1, TILES) as tile:
        for h in range(2):
            load_half(tile, h)
            load_squares(tile, h)

    def act_slot(tile, k):
        at = lagged(tile, k, 5)
        if at:
            t_, k_ = at
            done(A, s_cap, t_, k_, 1)
            A.activation(EX[k_ % 2][:], EX[k_ % 2][:], ACT.Ln, bias=half_col[:], scale=0.5).then_inc(s_ln, 1)
        at = lagged(tile, k, 4)
        if at:
            t_, k_ = at
            done(A, s_pre, t_, k_, 1)
            done(A, s_ssp, t_, k_, -1)
            A.activation(EX[k_ % 2][:], pre(k_ % 2), ACT.Exp, bias=cols["b1"][:]).then_inc(s_exp, 1)
        at = lagged(tile, k, 0)
        if at:
            h, r = k // 4, k % 4
            piece = slice(r * PIECE, (r + 1) * PIECE)
            if r == 0:
                A.wait_ge(s_adj[h], tile * 32 + 32)
                done(A, s_pre, tile, 4 * h, -4)
            A.activation(E[h][:, piece], E[h][:, piece], ACT.Square, bias=cols["off"][:]).then_inc(s_diff, 1)
            done(A, s_diff, tile, k, 1)
            A.activation(G[h][:, piece], E[h][:, piece], ACT.Exp, scale=COEFF).then_inc(s_gauss, 1)

    A.preload_act_table_set("natural_log_exp_and_others")
    pipeline(A, act_slot, 5)

    def pe_slot(tile, k):
        at = lagged(tile, k, 4)
        if at:
            t_, k_ = at
            h, b, c = parts(k_)
            done(PE, s_gauss, t_, 4 * h, 2 * c + 2)
            done(PE, s_ssp, t_, k_, -1)
            for n in range(2):
                last = PE.matmul(PS[:, 2 * (k_ % 2) + n, :], W1pad[:, b, :],
                                 G[h][:, c * CHUNK + n * BANK:c * CHUNK + (n + 1) * BANK], start=True, stop=True)
            last.then_inc(s_pre, 1)
        at = lagged(tile, k, 6)
        if at:
            t_, k_ = at
            done(PE, s_ssp, t_, k_, 1)
            done(PE, s_prod, t_, k_, -1)
            for n in range(2):
                last = PE.matmul(PS[:, 4 + 2 * (k_ % 2) + n, :], W2T[:],
                                 Hs[k_ % 2][:, n * BANK:(n + 1) * BANK], start=True, stop=True)
            last.then_inc(s_post, 1)

    pipeline(PE, pe_slot, 6)

    def i_major(ap):
        return ap.rearrange("p (i j) -> p i j", j=NODES)

    def gp_slot(tile, k):
        at = lagged(tile, k, 6)
        if at:
            t_, k_ = at
            h, b, c = parts(k_)
            GP.wait_ge(s_sq[h][b], t_ * 16 + 16)
            done(GP, s_prod, t_, k_, -1)
            GP.sem_inc(apart, 1)
            rf = rfT[:, bass.ds(t_ * P + b * NODES, NODES)].unsqueeze(1).broadcast_to([P, CHUNK // NODES, NODES])
            GP.tensor_tensor(i_major(GATE[k_ % 2][:]), rf, i_major(A2[h][b][:, c * CHUNK:(c + 1) * CHUNK]),
                             ALU.mult).then_inc(s_gate, 1)
        at = lagged(tile, k, 7)
        if at:
            t_, k_ = at
            done(GP, s_prod, t_, k_, 1)
            done(GP, s_sum, t_, k_, -1)
            product = i_major(PR[k_ % 2][:])
            GP.tensor_tensor(HP[k_ % 2][:].rearrange("p (i j) -> p i j", j=NODES // 2), product[:, :, 0:NODES // 2],
                             product[:, :, NODES // 2:], ALU.add).then_inc(s_half, 1)

    pipeline(GP, gp_slot, 7)

    def dve_slot(tile, k):
        at = lagged(tile, k, 5)
        if at:
            t_, k_ = at
            done(V, s_exp, t_, k_, 1)
            V.tensor_scalar(EX[k_ % 2][:], EX[k_ % 2][:], EXP_CAP, None, ALU.min).then_inc(s_cap, 1)
        at = lagged(tile, k, 7)
        if at:
            t_, k_ = at
            h, b, c = parts(k_)
            done(V, s_post, t_, k_, 1)
            done(V, s_gate, t_, k_, 1)
            done(V, s_half, t_, k_, -1)
            V.scalar_tensor_tensor(PR[k_ % 2][:], post(k_ % 2), cols["b2"][:], GATE[k_ % 2][:],
                                   ALU.add, ALU.mult).then_inc(s_prod, 1)
        at = lagged(tile, k, 5)
        if at:
            t_, k_ = at
            done(V, s_ln, t_, k_, 1)
            done(V, s_post, t_, k_, -1)
            V.scalar_tensor_tensor(Hs[k_ % 2][:], pre(k_ % 2), cols["b1l"][:], EX[k_ % 2][:],
                                   ALU.add, ALU.max).then_inc(s_ssp, 1)
        at = lagged(tile, k, 8)
        if at:
            t_, k_ = at
            h, b, c = parts(k_)
            done(V, s_half, t_, k_, 1)
            first = b * NODES + h * (NODES // 2) + c * (CHUNK // NODES)
            V.tensor_reduce(yT[:, bass.ds(t_ * P + first, CHUNK // NODES)],
                            HP[k_ % 2][:].rearrange("p (i j) -> p i j", j=NODES // 2), AX, ALU.add).then_inc(s_sum, 1)

    pipeline(V, dve_slot, 8)


DT = 8
DOT_GROUPS = TILES // DT


def attend_stage(nc, own, PS, apart, hw_d, hs_d, att_d, U, VT, w2sel, cols):
    V, A, PE, GP, SP = nc.vector, nc.scalar, nc.tensor, nc.gpsimd, nc.sync

    def sem(name):
        return own.enter_context(nc.semaphore(name))

    def sb(name, shape):
        return own.enter_context(nc.sbuf_tensor(name, shape, F32))

    Q = [sb(f"a_q{b}", [P, PAIRS]) for b in range(2)]
    QV, QU = sb("a_qv", [P, PAIRS]), sb("a_qu", [P, PAIRS])
    ST = [sb(f"a_w{b}", [P, P]) for b in range(2)]
    SI = [sb(f"a_silu{n}", [P, CHUNK]) for n in range(2)]
    W2 = [sb(f"a_w2{b}", [P, 2, 32]) for b in range(2)]
    ATT = sb("a_att", [P, BANK])
    VS, US = sb("a_vs", [P, NODES]), sb("a_us", [P, NODES])
    Z = 7
    att_out = att_d.rearrange("(g m q i) j -> g q m (i j)", g=DOT_GROUPS, q=4, i=BANK // NODES)

    s_w = [sem(f"s_w{b}") for b in range(2)]
    s_ones, s_v, s_u, s_q = sem("s_ones"), sem("s_v"), sem("s_u"), sem("s_q")
    s_vs, s_us = sem("s_vs"), sem("s_us")
    s_sel, s_first, s_silu, s_dot = sem("s_sel"), sem("s_first"), sem("s_silu"), sem("s_dot")
    s_tanh, s_out = sem("s_tanh"), sem("s_out")
    SILU_0, DOT_0, TANH_0, OUT_0, FIRST_0 = 2, 5, 1, 1, 5
    A.nop().then_inc(s_silu, SILU_0)
    PE.nop().then_inc(s_dot, DOT_0)
    PE.nop().then_inc(s_first, FIRST_0)
    A.nop().then_inc(s_tanh, TANH_0)
    SP.nop().then_inc(s_out, OUT_0)

    def rows_of(b):
        return slice(b * NODES, (b + 1) * NODES)

    def before(engine, s, count):
        if not isinstance(count, int) or count > 0:
            engine.wait_ge(s, count)

    def first_and_rest(engine, body):
        body(0)
        with engine.Fori(1, TILES) as tile:
            body(tile)

    def sp_tile(tile):
        for b in range(2):
            before(SP, s_first, (tile - 1) * 8 + (4 * b + 4 + FIRST_0))
            row = bass.ds(tile * P + b * NODES, NODES)
            SP.dma_start(ST[b][rows_of(b), :], hw_d[row, :]).then_inc(s_w[b], 16)
            SP.dma_start(ST[b][rows_of(1 - b), :], hs_d[row, :]).then_inc(s_w[b], 16)

    first_and_rest(SP, sp_tile)

    def by_pair(ap):
        return ap.rearrange("p (i j) -> p i j", j=NODES)

    square = [NODES, NODES, NODES]
    for b in range(2):
        GP.memset(Q[b][rows_of(1 - b), :], 1.0).then_inc(s_ones, 1)
    GP.wait_ge(s_ones, 2)
    for b in range(2):
        o = by_pair(Q[b][rows_of(1 - b), :])
        GP.affine_select(out=o, in_=o, compare_op=ALU.is_equal, fill=0.0, base=0,
                         pattern=[[-1, NODES], [0, NODES]], channel_multiplier=1).then_inc(s_ones, 1)

    def gp_tile(tile):
        for b in range(2):
            r = rows_of(b)
            before(GP, s_v, (tile - 1) * 2 + (b + 1))
            before(GP, s_u, (tile - 1) * 2 + (b + 1))
            GP.sem_inc(apart, 1)
            GP.tensor_copy(VS[r, :], VT[r, bass.ds(tile, 1), :].rearrange("p o i -> p (o i)")).then_inc(s_vs, 1)
            GP.tensor_copy(US[r, :], U[r, bass.ds(tile, 1), :].rearrange("p o j -> p (o j)")).then_inc(s_us, 1)
            before(GP, s_q, (tile - 1) * 2 + (b + 1))
            GP.wait_ge(s_vs, tile * 2 + (b + 1))
            GP.sem_inc(apart, 1)
            GP.affine_select(out=by_pair(QV[r, :]), in_=VS[r, :].unsqueeze(2).broadcast_to(square),
                             compare_op=ALU.is_equal, fill=0.0, base=0,
                             pattern=[[0, NODES], [-1, NODES]], channel_multiplier=1).then_inc(s_v, 1)
            GP.wait_ge(s_us, tile * 2 + (b + 1))
            GP.sem_inc(apart, 1)
            GP.affine_select(out=by_pair(QU[r, :]), in_=US[r, :].unsqueeze(1).broadcast_to(square),
                             compare_op=ALU.is_equal, fill=0.0, base=0,
                             pattern=[[-1, NODES], [0, NODES]], channel_multiplier=1).then_inc(s_u, 1)

    first_and_rest(GP, gp_tile)

    with V.Fori(0, DOT_GROUPS) as g:
        with V.Fori(0, DT) as tl:
            for b in range(2):
                r = rows_of(b)
                graphs = g * (2 * DT) + tl * 2 + (b + 1)
                V.wait_ge(s_v, graphs)
                V.wait_ge(s_u, graphs)
                V.wait_ge(s_first, g * (8 * DT) + tl * 8 + (4 * b + 4 - 8 + FIRST_0))
                V.tensor_tensor(Q[b][r, :], QV[r, :], QU[r, :], ALU.add).then_inc(s_q, 1)
                V.wait_ge(s_dot, g * (8 * DT) + tl * 8 + (4 * b + 4 - 8 + DOT_0))
                V.sem_inc(apart, 1)
                for c in range(2):
                    last = V.tensor_copy(W2[b][:, c, :], w2sel[:, bass.ds(32 - 2 * b - c - tl * 4, 32)])
                last.then_inc(s_sel, 1)

    def pe_slot(g, tl, k):
        n = g * (8 * DT) + (tl * 8 + k)
        if not isinstance(tl, int) or tl < DT:
            b, c = k // 4, k % 4
            if c == 0:
                PE.wait_ge(s_q, g * (2 * DT) + (tl * 2 + (b + 1)))
                PE.wait_ge(s_w[b], g * (32 * DT) + (tl * 32 + 32))
            PE.wait_ge(s_silu, n + (-1 + SILU_0))
            for m in range(2):
                last = PE.matmul(PS[:, 2 * (k % 2) + m, :], ST[b][:],
                                 Q[b][:, c * CHUNK + m * BANK:c * CHUNK + (m + 1) * BANK], start=True, stop=True)
            last.then_inc(s_first, 1)
        if isinstance(tl, int) and tl == 0 and k == 0:
            return
        tl, k = (tl, k - 1) if k else (tl - 1, 7)
        b, c = k // 4, k % 4
        head = isinstance(tl, int) and tl == 0 and k < 2
        if head and k == 0:
            PE.wait_ge(s_tanh, g + TANH_0)
        if c == 0:
            PE.wait_ge(s_sel, g * (2 * DT) + (tl * 2 + (b + 1)))
        PE.wait_ge(s_silu, n + (0 + SILU_0))
        for m in range(2):
            q = (2 * c + m) % 4
            last = PE.matmul(PS[32 * q:32 * q + 32, Z, :], W2[b][:, (2 * c + m) // 4, :],
                             SI[k % 2][:, m * BANK:(m + 1) * BANK], start=head, stop=True, skip_group_check=True)
        last.then_inc(s_dot, 1)

    PE.wait_ge(s_ones, 4)
    with PE.Fori(0, DOT_GROUPS) as g:
        for k in range(8):
            pe_slot(g, 0, k)
        with PE.Fori(1, DT) as tl:
            for k in range(8):
                pe_slot(g, tl, k)
        pe_slot(g, DT, 0)

    with A.Fori(0, DOT_GROUPS) as g:
        with A.Fori(0, DT) as tl:
            for k in range(8):
                n = g * (8 * DT) + tl * 8 + k
                A.wait_ge(s_first, n + (1 + FIRST_0))
                A.wait_ge(s_dot, n + (-1 + DOT_0))
                pre = PS[:, 2 * (k % 2):2 * (k % 2) + 2, :].rearrange("p b n -> p (b n)")
                A.activation(SI[k % 2][:], pre, ACT.Silu, bias=cols["att_b1"][:]).then_inc(s_silu, 1)
        A.wait_ge(s_dot, g * (8 * DT) + (8 * DT + DOT_0))
        A.wait_ge(s_out, g * 64 + OUT_0)
        A.activation(ATT[:], PS[:, Z, :], ACT.Tanh, scale=0.5, bias=cols["att_b2"][:]).then_inc(s_tanh, 1)
        A.wait_ge(s_tanh, g + (1 + TANH_0))
        for q in range(4):
            A.dma_start(att_out[bass.ds(g, 1), q, :, :].rearrange("o m n -> (o m) n"),
                        ATT[32 * q:32 * q + 32, :]).then_inc(s_out, 16)
    SP.wait_ge(s_out, DOT_GROUPS * 64 + OUT_0)


def kernel(**inputs):
    import numpy as _np
    import concourse.bacc as _bacc
    from concourse import mybir as _mybir
    from concourse.bass_utils import run_bass_kernel_spmd as _run

    turned = {"adj": "adjT", "L0_gnn_W1": "W1T", "L0_gnn_W2": "W2T", "L0_gnn_Wa": "WaT", "L0_gnn_Wd1": "Wd1T",
              "L0_gnn_Wd2": "Wd2T", "L1_gnn_W": "WT", "L1_gnn_att_w1": "WattT", "L1_gnn_mlp_w1": "Wm1T",
              "L1_gnn_mlp_w2": "Wm2T"}
    straight = ["x", "adj", "L0_gnn_b1", "L0_gnn_b2", "L0_gnn_bd1", "L0_gnn_bd2", "L1_gnn_b_lin",
                "L1_gnn_att_b1", "L1_gnn_att_w2", "L1_gnn_att_b2", "L1_gnn_mlp_b1", "L1_gnn_mlp_b2",
                "L2_gnn_W", "L2_gnn_b", "L3_gnn_W_msg", "L3_gnn_W_upd"]
    arrays = {n: _np.ascontiguousarray(inputs[n]) for n in straight}
    for n, name in turned.items():
        arrays[name] = _np.ascontiguousarray(_np.swapaxes(_np.asarray(inputs[n]), -1, -2))
    nc = _bacc.Bacc("TRN2", target_bir_lowering=False, num_devices=1)
    t = {n: nc.dram_tensor("in_" + n, a.shape, _mybir.dt.from_np(a.dtype), kind="ExternalInput").ap()
         for n, a in arrays.items()}
    out = nc.dram_tensor("out_x", arrays["x"].shape, _mybir.dt.float32, kind="ExternalOutput").ap()
    build(nc, t, out)
    r = _run(nc, [{"in_" + n: a for n, a in arrays.items()}], core_ids=[0])
    return r.results[0]["out_x"]
```

```python
from contextlib import ExitStack

import concourse.bass as bass
import numpy as np
from concourse import mybir

F32 = mybir.dt.float32
I32 = mybir.dt.int32
ALU = mybir.AluOpType
ACT = mybir.ActivationFunctionType
AX = mybir.AxisListType.X

P = 128
GRAPHS, NODES = 128, 64
NG = 64
CUTOFF = 5.0
TILES = GRAPHS // 2
PAIRS = NODES * NODES
BANK = 512
GT = 8
GROUPS = TILES // GT
GB = GT * P // BANK
CHAINS = 8 // (2 * GB)
LN2 = float(np.log(2.0))
OFFSETS = np.linspace(0.0, CUTOFF, NG, dtype=np.float32)
COEFF = float(np.float32(-0.5) / ((OFFSETS[1] - OFFSETS[0]) * (OFFSETS[1] - OFFSETS[0])))
EXP_CAP = 2.0 ** 60
MIN_NORM = 1e-15
MAX_NORM = 1.0 - 0.004
ONE_LESS = 1.0 - 1e-7
SMALL_SQ = 1.0 / 64
LN_EPS = 1e-5


class Chain:

    def __init__(self, nc, sem, name, apart):
        self.nc, self.sem, self.done, self.apart = nc, sem(name), 0, apart
        self.signals = {kind: sem(name + "_" + kind) for kind in ("load", "late", "store", "side")}
        self.signalled = {kind: 0 for kind in self.signals}
        self.first = []
        self.steps, self.per_turn = None, None

    def put(self, engine, emit, kind=None, turn=None, per=0, at=None, first=None):
        at = self.done if at is None else self.done + at
        if turn is not None:
            at = turn * per + at
        for s, count in [(self.sem, at)] * bool(turn is not None or at) + [
                (self.signals[k], n if turn is None else turn * self.per_turn[k] + n) for k, n in first]:
            engine.wait_ge(s, count)
            if turn is not None and engine is self.nc.sync:
                engine.sem_inc(self.apart, 1)
        if kind is None:
            emit().then_inc(self.sem, 1)
        else:
            emit(self.signals[kind])

    def step(self, engine, emit):
        first, self.first = self.first, []
        if self.steps is None:
            self.put(engine, emit, first=first)
            self.done += 1
        else:
            self.steps.append((engine, emit, None, self.count, first))
            self.count += 1

    def beside(self, kind, engine, emit, signals):
        if self.steps is None:
            self.put(engine, emit, kind, first=self.first)
        else:
            self.steps.append((engine, emit, kind, self.count, self.first))
        self.signalled[kind] += signals

    def side(self, engine, emit, after=False):
        kept = self.first
        if after:
            self.through("side")
        self.beside("side", engine, lambda s: emit().then_inc(s, 1), 1)
        self.first = kept

    def transfer(self, kind, pairs):
        self.beside(kind, self.nc.sync, lambda s: [self.nc.sync.dma_start(dst, src).then_inc(s, 16)
                                                   for dst, src in pairs], 16 * len(pairs))

    def through(self, kind):
        self.first = self.first + [(kind, self.signalled[kind])]

    def write(self, body, turn, n):
        before = dict(self.signalled)
        self.steps, self.count = [], 0
        body(turn, n)
        steps, self.steps = self.steps, None
        self.per_turn = {kind: self.signalled[kind] - before[kind] for kind in before}
        self.signalled = before
        return steps


def loop_together(nc, turns, chains, body):
    with nc.Fori(0, turns) as turn:
        lists = [c.write(body, turn, n) for n, c in enumerate(chains)]
        for steps in zip(*lists):
            for c, (engine, emit, kind, at, first) in zip(chains, steps):
                c.put(engine, emit, kind, turn, c.count, at, first)
    for c in chains:
        c.done += turns * c.count
        for kind in c.signalled:
            c.signalled[kind] += turns * c.per_turn[kind]


def build(nc, t, out):
    V, A, PE, GP, SP = nc.vector, nc.scalar, nc.tensor, nc.gpsimd, nc.sync
    ctx = ExitStack()
    with ctx:
        def sem(name):
            return ctx.enter_context(nc.semaphore(name))

        def sb(name, shape, dt=F32, where=ctx):
            return where.enter_context(nc.sbuf_tensor(name, shape, dt))

        def dram(name, shape):
            return nc.dram_tensor(name, shape, F32, kind="Internal").ap()

        PS = ctx.enter_context(nc.psum_tensor("PS", [P, 8, BANK], F32))

        def tiles(ap):
            return ap.rearrange("(t p) d -> p t d", p=P)

        x_in = tiles(t["x"].rearrange("b n d -> (b n) d"))
        x_out = tiles(out.rearrange("b n d -> (b n) d"))
        adj_pairs = t["adj"].rearrange("b i j -> b (i j)")
        adj_rows = tiles(t["adj"].rearrange("b i j -> (b i) j"))
        adjT_rows = tiles(t["adjT"].rearrange("b j i -> (b j) i"))
        adj_sq = dram("adj_sq", [GRAPHS, PAIRS])
        x1_d = dram("x1_d", [GRAPHS * NODES, P])
        h_d = dram("h_d", [GRAPHS * NODES, P])
        hw_d = dram("hw_d", [GRAPHS * NODES, P])
        hs_d = dram("hs_d", [GRAPHS * NODES, P])
        att_d = dram("att_d", [GRAPHS * NODES, NODES])

        apart = sem("apart")
        chains = [Chain(nc, sem, f"chain_{n}", apart) for n in range(CHAINS)]
        cur = [chains[0], 0]

        def v(emit): cur[0].step(V, emit)
        def a(emit): cur[0].step(A, emit)
        def pe(emit): cur[0].step(PE, emit)
        def gp(emit): cur[0].step(GP, emit)

        def together(body):
            def one(turn, n):
                cur[0], cur[1] = chains[n], n
                body(turn * CHAINS + n, n)
            loop_together(nc, GROUPS // CHAINS, chains, one)
            cur[0], cur[1] = chains[0], 0
            for c in chains:
                c.through("side")
                if c.signalled["store"]:
                    c.through("store")
                c.step(SP, lambda: SP.nop())

        def load(pairs):
            cur[0].transfer("load", pairs)
            cur[0].through("load")

        def store(pairs): cur[0].transfer("store", pairs)
        def stored(): cur[0].through("store")
        def beside(): cur[0].through("side")

        def const(name, shape):
            return sb(name, shape)

        W = {n: const("w_" + n, [P, P]) for n in
             ("WaT", "W2T", "Wd1T", "Wd2T", "WT", "Wm1LT", "Wm1RT", "Wm2T", "Wg", "Wmsg_s", "Wmsg_r", "Wub", "WsT", "WrT")}
        WrlT = const("WrlT", [P, 2 * P])
        W3 = const("W3", [P, 3 * P])
        W1pad = const("W1pad", [P, 2, P])
        w2sel = const("w2sel", [P, 64])
        cols = {n: const("c_" + n, [P, 1]) for n in
                ("b1", "b1l", "b2", "bd1", "bd1l", "att_b1", "mlp_b1", "att_w2", "att_b2", "off", "hb2")}
        rows = {n: const("r_" + n, [P, P]) for n in ("bd2", "hb", "mlp_b2", "L2_b")}
        ident = const("ident", [P, P])
        ones = const("ones", [P, NODES])
        big = sb("big", [P, TILES * P + NODES])
        rfT = big
        x2_all = const("x2_all", [P, TILES])
        cs_all = const("cs_all", [P, TILES])
        smalls = [const(f"small{n}", [P, 30, GT]) for n in range(CHAINS)]
        tmpc = const("tmpc", [P, 8])
        half_col = const("half_col", [P, 1])
        off_i = sb("off_i", [P, 1], I32)

        gp(lambda: GP.memset(ident[:], 0.0))
        gp(lambda: GP.affine_select(out=ident[:], in_=ident[:], compare_op=ALU.not_equal, fill=1.0,
                                    base=0, pattern=[[-1, P]], channel_multiplier=1))
        gp(lambda: GP.memset(ones[:], 1.0))
        gp(lambda: GP.memset(big[:, TILES * P:], 0.0))
        gp(lambda: GP.memset(W1pad[:], 0.0))
        gp(lambda: GP.memset(w2sel[:], 0.0))
        gp(lambda: GP.iota(off_i[0:NG, :], [[0, 1]], base=0, channel_multiplier=1))
        gp(lambda: GP.iota(off_i[NG:P, :], [[0, 1]], base=0, channel_multiplier=1))

        def column(ap):
            return ap.rearrange("(p o) -> p o", o=1)

        def across(ap):
            return ap.rearrange("(o n) -> o n", o=1).broadcast_to([P, ap.shape[0]])

        load([
            (W["WaT"][:], t["WaT"]), (W["W2T"][:], t["W2T"]), (W["Wd1T"][:], t["Wd1T"]),
            (W["Wd2T"][:], t["Wd2T"]), (W["WT"][:], t["WT"]), (W["Wm2T"][:], t["Wm2T"]),
            (W["Wm1LT"][:], t["Wm1T"][0:P, :]), (W["Wm1RT"][:], t["Wm1T"][P:2 * P, :]),
            (W["Wg"][:], t["L2_gnn_W"]),
            (W["Wmsg_s"][:], t["L3_gnn_W_msg"][0:P, :]), (W["Wmsg_r"][:], t["L3_gnn_W_msg"][P:2 * P, :]),
            (W["Wub"][:], t["L3_gnn_W_upd"][P:2 * P, :]), (W3[:, P:2 * P], t["L3_gnn_W_upd"][0:P, :]),
            (WrlT[:, 0:P], t["WattT"][P:2 * P, :]), (WrlT[:, P:2 * P], t["WattT"][0:P, :]),
            (W1pad[0:NG, 0, :], t["W1T"]), (W1pad[NG:P, 1, :], t["W1T"]),
            (cols["b1"][:], column(t["L0_gnn_b1"])), (cols["b2"][:], column(t["L0_gnn_b2"])),
            (cols["bd1"][:], column(t["L0_gnn_bd1"])), (cols["att_b1"][:], column(t["L1_gnn_att_b1"])),
            (cols["mlp_b1"][:], column(t["L1_gnn_mlp_b1"])),
            (cols["att_w2"][:], t["L1_gnn_att_w2"].rearrange("o p -> p o")),
            (cols["att_b2"][:], across(t["L1_gnn_att_b2"])),
            (rows["bd2"][:], across(t["L0_gnn_bd2"])), (rows["hb"][:], across(t["L1_gnn_b_lin"])),
            (rows["mlp_b2"][:], across(t["L1_gnn_mlp_b2"])), (rows["L2_b"][:], across(t["L2_gnn_b"])),
        ])
        early = ExitStack()
        ad = sb("ad", [P, PAIRS], where=early)
        chains[0].transfer("late", [(ad[:], adj_pairs)])
        v(lambda: V.tensor_copy(w2sel[:, 32:33], cols["att_w2"][:]))
        v(lambda: V.tensor_copy(cols["off"][:], off_i[:]))
        v(lambda: V.tensor_scalar(cols["off"][:], cols["off"][:], -CUTOFF, 1.0 / (NG - 1), ALU.mult, ALU.mult))
        v(lambda: V.tensor_scalar(cols["b1l"][:], cols["b1"][:], -LN2, None, ALU.add))
        v(lambda: V.tensor_scalar(cols["bd1l"][:], cols["bd1"][:], -LN2, None, ALU.add))
        v(lambda: V.tensor_scalar(cols["att_b2"][:], cols["att_b2"][:], 0.5, None, ALU.mult))

        pe(lambda: PE.transpose(PS[:, 0, 0:P], W["Wmsg_s"][:], ident[:]))
        pe(lambda: PE.transpose(PS[:, 1, 0:P], W["Wmsg_r"][:], ident[:]))
        v(lambda: V.tensor_copy(W["WsT"][:], PS[:, 0, 0:P]))
        v(lambda: V.tensor_copy(W["WrT"][:], PS[:, 1, 0:P]))
        pe(lambda: PE.matmul(PS[:, 0, 0:P], W["WsT"][:], W["Wub"][:], start=True, stop=True))
        pe(lambda: PE.matmul(PS[:, 1, 0:P], W["WrT"][:], W["Wub"][:], start=True, stop=True))
        v(lambda: V.tensor_copy(W3[:, 0:P], PS[:, 0, 0:P]))
        v(lambda: V.tensor_copy(W3[:, 2 * P:3 * P], PS[:, 1, 0:P]))

        def ts(o, i, s1, op0, s2=None, op1=None):
            if op1 is None:
                v(lambda: V.tensor_scalar(o, i, s1, None, op0))
            else:
                v(lambda: V.tensor_scalar(o, i, s1, s2, op0, op1))

        def tt(o, x, y, op):
            v(lambda: V.tensor_tensor(o, x, y, op))

        def stt(o, x, s, y, op0, op1):
            v(lambda: V.scalar_tensor_tensor(o, x, s, y, op0, op1))

        def recip(o, i):
            v(lambda: V.reciprocal(o, i))

        def act(o, i, f, scale=1.0, bias=0.0):
            a(lambda: A.activation(o, i, f, bias=bias, scale=scale))

        def rsum(o, i):
            v(lambda: V.tensor_reduce(o, i, AX, ALU.add))

        def series(o, q):
            ts(o, q, 1.0 / 11, ALU.mult)
            for d in (9, 7, 5, 3):
                stt(o, o, 1.0 / d, q, ALU.add, ALU.mult)
            ts(o, o, 1.0, ALU.add)

        def artanh_over(o, q, z, ratio, m, w):
            act(w, ratio, ACT.Ln)
            ts(m, z, 0.1, ALU.max)
            recip(m, m)
            stt(w, w, 0.5, m, ALU.mult, ALU.mult)
            series(o, q)
            tt(w, w, o, ALU.subtract)
            ts(m, q, SMALL_SQ, ALU.is_ge)
            tt(w, w, m, ALU.mult)
            tt(o, o, w, ALU.add)

        def artanh(o, z, q, ratio, m, w):
            ts(m, z, -1.0, ALU.mult, 1.0, ALU.add)
            recip(m, m)
            stt(ratio, z, 1.0, m, ALU.add, ALU.mult)
            tt(q, z, z, ALU.mult)
            artanh_over(o, q, z, ratio, m, w)
            tt(o, o, z, ALU.mult)

        with ExitStack() as c0:
            sq = sb("sq0", [P, P], where=c0)
            tt(sq[:], rows["hb"][:], rows["hb"][:], ALU.mult)
            rsum(tmpc[:, 0:1], sq[:])
            act(tmpc[:, 1:2], tmpc[:, 0:1], ACT.Sqrt)
            ts(tmpc[:, 1:2], tmpc[:, 1:2], MIN_NORM, ALU.max)
            recip(tmpc[:, 2:3], tmpc[:, 1:2])
            act(tmpc[:, 3:4], tmpc[:, 1:2], ACT.Tanh)
            ts(tmpc[:, 3:4], tmpc[:, 3:4], MAX_NORM, ALU.min)
            tt(tmpc[:, 3:4], tmpc[:, 3:4], tmpc[:, 2:3], ALU.mult)
            ts(rows["hb"][:], rows["hb"][:], tmpc[:, 3:4], ALU.mult)
            tt(sq[:], rows["hb"][:], rows["hb"][:], ALU.mult)
            rsum(cols["hb2"][:], sq[:])

            chains[0].through("late")
            tt(ad[:], ad[:], ad[:], ALU.mult)
            store([(adj_sq, ad[:])])

        def bc(col):
            return col.unsqueeze(2).broadcast_to([P, GT, P])

        def brow(row):
            return row[:].unsqueeze(1).broadcast_to([P, GT, P])

        def flat(buf):
            return buf[:].rearrange("p t d -> p (t d)")

        def S(n):
            return smalls[cur[1]][:, n, :]

        def place(n, width=P):
            first = (2 * cur[1] + n) * GB
            return PS[:, first:first + GB * width // P, :].rearrange("p b (t d) -> p (b t) d", d=width)

        def columns(n):
            return place(n).rearrange("p t d -> p (t d)")

        def norm_relu(X, XC, SQ, H, extra=None, read_beside=False):
            rsum(S(0), X[:])
            ts(S(0), S(0), 1.0 / P, ALU.mult)
            tt(XC[:], X[:], bc(S(0)), ALU.subtract)
            squares(S(1), XC, SQ)
            ts(S(1), S(1), 1.0 / P, ALU.mult, LN_EPS, ALU.add)
            act(S(1), S(1), ACT.Sqrt)
            recip(S(1), S(1))
            if extra is not None:
                tt(S(1), S(1), extra, ALU.mult)
            if read_beside:
                beside()
            stt(H[:], XC[:], 0.0, bc(S(1)), ALU.max, ALU.mult)

        def turn_tiles(SRC, n, DST, beside=False):
            to = place(n)

            def go():
                for k in range(GT):
                    last = PE.transpose(to[:, k, :], SRC[:, k, :], ident[:])
                return last
            if beside:
                copy, sums = flat(DST), columns(n)
                cur[0].side(PE, go, after=True)
                cur[0].side(A, lambda: A.activation(copy, sums, ACT.Copy), after=True)
                return
            pe(go)
            act(flat(DST), columns(n), ACT.Copy)

        def wide(at, parts, beside=False):
            to = columns(at)

            def go():
                for c in range(GB):
                    for n, (w, cols_of) in enumerate(parts):
                        last = PE.matmul(to[:, c * BANK:(c + 1) * BANK], w, cols_of(c),
                                         start=n == 0, stop=n == len(parts) - 1)
                return last
            if beside:
                cur[0].side(PE, go, after=True)
            else:
                pe(go)

        def half(buf):
            return lambda c: flat(buf)[:, c * BANK:(c + 1) * BANK]

        def per_tile(n, lhs, rhs, width=P):
            region = place(n, width)

            def go():
                for k in range(GT):
                    last = PE.matmul(region[:, k, :], lhs(k), rhs(k), start=True, stop=True)
                return last
            pe(go)
            return region

        def ssp(o, i, bias, bias_l):
            act(o, i, ACT.Exp, bias=bias)
            ts(o, o, EXP_CAP, ALU.min)
            act(o, o, ACT.Ln, scale=0.5, bias=half_col[:])
            stt(o, i, bias_l, o, ALU.add, ALU.max)

        v(lambda: V.memset(half_col[:], 0.5))

        def squares(o, X, SQ):
            act(SQ[:], X[:], ACT.Square)
            rsum(o, SQ[:])

        def side(o, x, y, op):
            cur[0].side(GP, lambda: GP.tensor_tensor(o, x, y, op))

        def buffers(names, tag, where, width=P):
            return [[sb(f"{n}{tag}{c}", [P, GT, width], where=where) for n in names] for c in range(CHAINS)]

        with ExitStack() as c1:
            bufs = buffers(("X", "XC", "SQ", "H", "HT"), "1", c1)

            def prepare(g, n):
                X, XC, SQ, H, HT = bufs[n]
                load([(X[:], x_in[:, bass.ds(g * GT, GT), :])])
                norm_relu(X, XC, SQ, H, read_beside=True)
                turn_tiles(H, 0, HT, beside=True)
                wide(1, [(W["WaT"][:], half(HT))], beside=True)
                rf, sums = rfT[:, bass.ds(g * (GT * P), GT * P)], columns(1)
                cur[0].side(A, lambda: A.activation(rf, sums, ACT.Copy), after=True)

            for c in chains:
                c.side(SP, lambda: SP.nop())
            for c in chains[1:]:
                c.step(SP, lambda: SP.nop())
            together(prepare)
        early.close()
        nc.all_engine_barrier()

        yT = sb("yT", [P, TILES * P])
        with ExitStack() as c2:
            filter_stage(nc, c2, PS, apart, adj_pairs, adj_sq, rfT, yT, W1pad, W["W2T"], cols, half_col)
        nc.all_engine_barrier()

        U = big[:, 0:TILES * NODES].rearrange("p (t j) -> p t j", j=NODES)
        VT = big[:, TILES * NODES:2 * TILES * NODES].rearrange("p (t j) -> p t j", j=NODES)
        VP = sb("VP", [P, TILES, NODES])
        with ExitStack() as c3:
            bufs = buffers(("X", "XC", "SQ", "H", "HT", "MX"), "3", c3)
            pair_bufs = buffers(("y2", "a1", "den", "n1", "q", "z", "m", "w", "T", "oy"), "q", c3, NODES)

            def between(g, n):
                X, XC, SQ, H, HT, MX = bufs[n]
                y2, a1, den, n1, q, z, m, w, T, oy = (x[:] for x in pair_bufs[n])
                nodes = bass.ds(g * GT, GT)
                stored()
                cur[0].transfer("late", [(X[:], x_in[:, nodes, :])])
                to = columns(0)
                pe(lambda: [PE.matmul(to[:, c * BANK:(c + 1) * BANK], W["Wd1T"][:],
                                      yT[:, bass.ds(g * (GT * P) + c * BANK, BANK)],
                                      start=True, stop=True) for c in range(GB)][-1])
                ssp(flat(HT), columns(0), cols["bd1"][:], cols["bd1l"][:])
                cur[0].through("late")
                side(X[:], X[:], brow(rows["bd2"]), ALU.add)
                y3 = per_tile(1, lambda k: HT[:, k, :], lambda k: W["Wd2T"][:])
                beside()
                tt(X[:], y3, X[:], ALU.add)
                store([(tiles(x1_d)[:, nodes, :], X[:])])
                norm_relu(X, XC, SQ, H)
                side(SQ[:], H[:], H[:], ALU.mult)
                turn_tiles(H, 0, HT)
                mx = per_tile(1, lambda k: HT[:, k, :], lambda k: W["WT"][:])
                act(MX[:], mx, ACT.Copy)
                beside()
                rsum(S(2), SQ[:])
                side(XC[:], MX[:], brow(rows["hb"]), ALU.mult)
                squares(S(3), MX, SQ)
                act(S(5), S(2), ACT.Sqrt)
                act(S(6), S(3), ACT.Sqrt)
                ts(S(5), S(5), MIN_NORM, ALU.max)
                ts(S(6), S(6), MIN_NORM, ALU.max)
                ts(S(7), S(5), ONE_LESS, ALU.min)
                artanh(S(8), S(7), S(9), S(10), S(11), S(12))
                recip(S(13), S(5))
                recip(S(14), S(6))
                tt(S(8), S(8), S(13), ALU.mult)
                tt(S(8), S(8), S(6), ALU.mult)
                act(S(8), S(8), ACT.Tanh)
                ts(S(8), S(8), MAX_NORM, ALU.min)
                tt(S(8), S(8), S(14), ALU.mult)
                tt(S(15), S(8), S(8), ALU.mult)
                tt(S(15), S(15), S(3), ALU.mult)
                beside()
                rsum(S(4), XC[:])
                tt(S(16), S(8), S(4), ALU.mult)
                ts(S(16), S(16), 2.0, ALU.mult, 1.0, ALU.add)
                stt(S(17), S(15), cols["hb2"][:], S(16), ALU.mult, ALU.add)
                ts(S(17), S(17), MIN_NORM, ALU.max)
                recip(S(17), S(17))
                ts(S(15), S(15), -1.0, ALU.mult, 1.0, ALU.add)
                tt(S(15), S(15), S(17), ALU.mult)
                side(SQ[:], brow(rows["hb"]), bc(S(15)), ALU.mult)
                stt(S(16), S(16), cols["hb2"][:], S(8), ALU.add, ALU.mult)
                tt(S(16), S(16), S(17), ALU.mult)
                tt(H[:], MX[:], bc(S(16)), ALU.mult)
                beside()
                tt(H[:], H[:], SQ[:], ALU.add)
                squares(S(18), H, SQ)
                act(S(19), S(18), ACT.Sqrt)
                ts(S(19), S(19), MIN_NORM, ALU.max)
                recip(S(19), S(19))
                ts(S(19), S(19), MAX_NORM, ALU.mult, 1.0, ALU.min)
                tt(H[:], H[:], bc(S(19)), ALU.mult)
                turn_tiles(H, 0, HT, beside=True)
                squares(S(20), H, SQ)
                x2, x2_1 = S(20), S(21)
                v(lambda: V.tensor_copy(x2_all[:, nodes], x2))
                ts(x2_1, x2, -1.0, ALU.mult, 1.0, ALU.add)
                ts(S(22), x2, -2.0, ALU.mult, 1.0, ALU.add)
                tt(S(23), S(22), x2, ALU.add)
                tt(S(23), x2_1, S(23), ALU.subtract)
                tt(S(24), x2, x2, ALU.mult)
                tt(S(24), S(24), S(22), ALU.add)
                recip(S(24), S(24))
                tt(S(23), S(23), S(24), ALU.mult)
                tt(S(24), S(23), S(23), ALU.mult)
                tt(S(24), S(24), x2, ALU.mult)
                series(S(25), S(24))
                tt(S(25), S(25), S(23), ALU.mult)
                tt(S(25), S(25), x2_1, ALU.mult)
                cs = S(25)
                v(lambda: V.tensor_copy(cs_all[:, nodes], cs))
                beside()
                r = per_tile(0, lambda k: HT[:, k, :], lambda k: WrlT[:], 2 * P)
                act(XC[:], r[:, :, 0:P], ACT.Copy)
                tt(SQ[:], r[:, :, P:2 * P], bc(cs), ALU.mult)
                store([(tiles(h_d)[:, nodes, :], H[:]), (tiles(hw_d)[:, nodes, :], XC[:]),
                       (tiles(hs_d)[:, nodes, :], SQ[:])])
                act(MX[:], HT[:], ACT.Square)
                first = 2 * GB * cur[1]

                def dots():
                    for k in range(GT):
                        for b in range(2):
                            ri = slice(b * NODES, (b + 1) * NODES)
                            cj = slice(k * NODES, (k + 1) * NODES)
                            PE.matmul(PS[ri, first, cj], HT[:, k, ri], HT[:, k, ri], start=True, stop=True)
                            last = PE.matmul(PS[ri, first + 1, cj], ones[:], MX[:, k, ri], start=True, stop=True)
                    return last
                pe(dots)
                G = PS[:, first, 0:GT * NODES].rearrange("p (t j) -> p t j", j=NODES)
                Y2 = PS[:, first + 1, 0:GT * NODES].rearrange("p (t j) -> p t j", j=NODES)

                def of_i(col):
                    return col.unsqueeze(2).broadcast_to([P, GT, NODES])
                act(y2, Y2, ACT.Copy)
                side(den, y2, of_i(x2), ALU.mult)
                ts(oy, y2, -1.0, ALU.mult, 1.0, ALU.add)
                side(m, oy, of_i(x2_1), ALU.mult)
                ts(a1, G, -2.0, ALU.mult, 1.0, ALU.add)
                stt(q, G, -2.0, y2, ALU.mult, ALU.add)
                tt(q, q, of_i(x2), ALU.add)
                beside()
                tt(den, den, a1, ALU.add)
                side(n1, a1, y2, ALU.add)
                ts(den, den, MIN_NORM, ALU.max)
                tt(T, den, m, ALU.mult)
                recip(T, T)
                beside()
                tt(a1, T, m, ALU.mult)
                stt(q, q, 0.0, a1, ALU.max, ALU.mult)
                side(oy, oy, oy, ALU.mult)
                act(z, q, ACT.Sqrt)
                tt(m, T, den, ALU.mult)
                tt(m, m, den, ALU.mult)
                stt(w, z, 1.0, m, ALU.add, ALU.mult)
                stt(w, z, 1.0, w, ALU.add, ALU.mult)
                artanh_over(T, q, z, w, m, w)
                tt(T, T, a1, ALU.mult)
                beside()
                tt(VT[:, nodes, :], oy, T, ALU.mult)
                tt(m, T, of_i(x2_1), ALU.mult)
                tt(VP[:, nodes, :], m, of_i(x2_1), ALU.mult)
                stt(U[:, nodes, :], m, -1.0, n1, ALU.mult, ALU.mult)

            together(between)
        nc.all_engine_barrier()

        with ExitStack() as c4:
            attend_stage(nc, c4, PS, apart, hw_d, hs_d, att_d, big, w2sel, cols)
        nc.all_engine_barrier()

        with ExitStack() as c5:
            bufs = buffers(("X", "XC", "SQ", "H", "ST", "UU", "AV", "AB", "ABT"), "5", c5)
            pair_bufs = buffers(("at", "am"), "p", c5, NODES)
            for c in range(CHAINS):
                for buf in bufs[c][-3:]:
                    v(lambda buf=buf: V.memset(buf[:], 0.0))
            nc.all_engine_barrier()

            def two_blocks(buf):
                return [(slice(0, NODES), buf[0:NODES, :, 0:NODES]), (slice(NODES, P), buf[NODES:P, :, NODES:P])]

            def finish(g, n):
                X, XC, SQ, H, ST, UU, AV, AB, ABT = bufs[n]
                at, am = pair_bufs[n]
                nodes = bass.ds(g * GT, GT)
                cur[0].transfer("load", [(at[:], tiles(att_d)[:, nodes, :]), (am[:], adj_rows[:, nodes, :]),
                                         (H[:], tiles(h_d)[:, nodes, :])])
                stored()
                cur[0].transfer("late", [(X[:], tiles(x1_d)[:, nodes, :])]
                                + [(blk, adj_rows[r, nodes, :]) for r, blk in two_blocks(AB)]
                                + [(blk, adjT_rows[r, nodes, :]) for r, blk in two_blocks(ABT)])
                cur[0].through("load")
                ts(at[:], at[:], 0.5, ALU.mult, 0.5, ALU.add)
                side(UU[:], H[:], bc(cs_all[:, nodes]), ALU.mult)
                turn_tiles(UU, 1, SQ, beside=True)
                tt(am[:], am[:], at[:], ALU.mult)
                tt(at[:], am[:], U[:, nodes, :], ALU.mult)
                rsum(S(0), at[:])
                for r, blk in two_blocks(AV):
                    tt(blk, am[r, :, :], VP[r, nodes, :], ALU.mult)
                small = smalls[cur[1]]
                v(lambda: [V.scalar_tensor_tensor(AV[:, k, :], ident[:], small[:, 0, k:k + 1], AV[:, k, :],
                                                  ALU.mult, ALU.add) for k in range(GT)][-1])
                turn_tiles(AV, 0, XC)
                beside()
                sup = per_tile(1, lambda k: H[:, k, :], lambda k: XC[:, k, :])
                act(ST[:], sup, ACT.Copy)
                side(UU[:], UU[:], brow(rows["mlp_b2"]), ALU.add)
                wide(1, [(W["Wm1LT"][:], half(SQ)), (W["Wm1RT"][:], half(ST))])
                act(flat(ST), columns(1), ACT.Silu, bias=cols["mlp_b1"][:])
                z2 = per_tile(0, lambda k: ST[:, k, :], lambda k: W["Wm2T"][:])
                beside()
                tt(UU[:], z2, UU[:], ALU.add)
                side(XC[:], H[:], UU[:], ALU.mult)
                squares(S(1), UU, SQ)
                x2 = S(3)
                v(lambda: V.tensor_copy(x2, x2_all[:, nodes]))
                ts(S(4), S(3), -1.0, ALU.mult, 1.0, ALU.add)
                act(S(5), S(1), ACT.Sqrt)
                ts(S(5), S(5), MIN_NORM, ALU.max)
                ts(S(6), S(4), MIN_NORM, ALU.max)
                recip(S(6), S(6))
                tt(S(6), S(6), S(5), ALU.mult)
                act(S(6), S(6), ACT.Tanh)
                recip(S(7), S(5))
                tt(S(6), S(6), S(7), ALU.mult)
                tt(S(8), S(6), S(6), ALU.mult)
                tt(S(8), S(8), S(1), ALU.mult)
                beside()
                rsum(S(2), XC[:])
                tt(S(9), S(6), S(2), ALU.mult)
                ts(S(9), S(9), 2.0, ALU.mult, 1.0, ALU.add)
                tt(S(10), S(8), S(3), ALU.mult)
                tt(S(10), S(10), S(9), ALU.add)
                ts(S(10), S(10), MIN_NORM, ALU.max)
                recip(S(10), S(10))
                tt(S(4), S(4), S(6), ALU.mult)
                tt(S(4), S(4), S(10), ALU.mult)
                side(UU[:], UU[:], bc(S(4)), ALU.mult)
                tt(S(9), S(9), S(8), ALU.add)
                tt(S(9), S(9), S(10), ALU.mult)
                tt(H[:], H[:], bc(S(9)), ALU.mult)
                beside()
                tt(H[:], H[:], UU[:], ALU.add)
                squares(S(11), H, SQ)
                act(S(12), S(11), ACT.Sqrt)
                ts(S(13), S(12), MIN_NORM, ALU.max)
                recip(S(14), S(13))
                ts(S(14), S(14), MAX_NORM, ALU.mult, 1.0, ALU.min)
                tt(S(15), S(13), S(14), ALU.mult)
                ts(S(15), S(15), MIN_NORM, ALU.max)
                ts(S(16), S(15), ONE_LESS, ALU.min)
                artanh(S(17), S(16), S(18), S(19), S(20), S(21))
                recip(S(15), S(15))
                tt(S(17), S(17), S(15), ALU.mult)
                tt(S(17), S(17), S(14), ALU.mult)
                tt(H[:], H[:], bc(S(17)), ALU.mult)
                act(H[:], H[:], ACT.Silu)
                squares(S(22), H, SQ)
                act(S(23), S(22), ACT.Sqrt)
                ts(S(23), S(23), MIN_NORM, ALU.max)
                recip(S(24), S(23))
                act(S(23), S(23), ACT.Tanh)
                ts(S(23), S(23), MAX_NORM, ALU.min)
                tt(S(23), S(23), S(24), ALU.mult)
                tt(H[:], H[:], bc(S(23)), ALU.mult)
                cur[0].through("late")
                tt(X[:], X[:], H[:], ALU.add)
                rsum(S(25), AB[:])
                ts(S(25), S(25), 1e-8, ALU.add)
                act(S(25), S(25), ACT.Sqrt)
                recip(S(25), S(25))
                norm_relu(X, XC, SQ, H, extra=S(25))
                side(X[:], X[:], brow(rows["L2_b"]), ALU.add)
                sup = per_tile(0, lambda k: H[:, k, :], lambda k: ABT[:, k, :])
                act(ST[:], sup, ACT.Copy)
                y = per_tile(1, lambda k: ST[:, k, :], lambda k: W["Wg"][:])
                tt(SQ[:], y, bc(S(25)), ALU.mult)
                beside()
                tt(X[:], X[:], SQ[:], ALU.add)
                norm_relu(X, XC, SQ, H)
                turn_tiles(H, 0, UU)
                rsum(S(26), ABT[:])
                ts(S(27), S(26), 0.0, ALU.is_gt)
                ts(S(26), S(26), 1.0, ALU.max)
                recip(S(26), S(26))
                tt(S(26), S(26), S(27), ALU.mult)
                y = per_tile(0, lambda k: UU[:, k, :], lambda k: W3[:, 0:2 * P], 2 * P)
                act(XC[:], y[:, :, 0:P], ACT.Copy)
                tt(X[:], y[:, :, P:2 * P], X[:], ALU.add)
                y = per_tile(0, lambda k: UU[:, k, :], lambda k: W3[:, 2 * P:3 * P])
                tt(SQ[:], y, bc(S(27)), ALU.mult)
                side(X[:], X[:], SQ[:], ALU.add)
                y = per_tile(1, lambda k: AB[:, k, :], lambda k: XC[:, k, :])
                tt(H[:], y, bc(S(26)), ALU.mult)
                beside()
                tt(X[:], X[:], H[:], ALU.add)
                store([(x_out[:, nodes, :], X[:])])

            together(finish)
        nc.all_engine_barrier()


CHUNK = 1024
SLOTS = 8
HALF = PAIRS // 2
N_CHUNKS = TILES * SLOTS


def pipeline(engine, slot, lag):
    for k in range(SLOTS):
        slot(0, k)
    with engine.Fori(1, TILES) as tile:
        for k in range(SLOTS):
            slot(tile, k)
    for k in range(lag):
        slot(TILES, k)


def lagged(tile, k, lag):
    k -= lag
    if k < 0:
        tile, k = tile - 1, k + SLOTS
    if isinstance(tile, int) and not 0 <= tile < TILES:
        return None
    return tile, k


def filter_stage(nc, own, PS, apart, adj_pairs, adj_sq, rfT, yT, W1pad, W2T, cols, half_col):
    V, A, PE, GP, SP = nc.vector, nc.scalar, nc.tensor, nc.gpsimd, nc.sync

    def sem(name):
        return own.enter_context(nc.semaphore(name))

    def sb(name, shape):
        return own.enter_context(nc.sbuf_tensor(name, shape, F32))

    E = [sb(f"f_adj{h}", [P, HALF]) for h in range(2)]
    G = [sb(f"f_gauss{h}", [P, HALF]) for h in range(2)]
    A2 = [[sb(f"f_sq{h}{b}", [P, HALF]) for b in range(2)] for h in range(2)]
    EX = [sb(f"f_ex{n}", [P, CHUNK]) for n in range(2)]
    Hs = [sb(f"f_h{n}", [P, CHUNK]) for n in range(2)]
    GATE = [sb(f"f_gate{n}", [P, CHUNK]) for n in range(2)]
    PR = [sb(f"f_prod{n}", [P, CHUNK]) for n in range(2)]
    HP = [sb(f"f_half{n}", [P, CHUNK // 2]) for n in range(2)]
    PIECE = BANK

    def pre(n):
        return PS[:, 2 * n:2 * n + 2, :].rearrange("p b n -> p (b n)")

    def post(n):
        return PS[:, 4 + 2 * n:6 + 2 * n, :].rearrange("p b n -> p (b n)")

    s_adj = [sem(f"s_adj{h}") for h in range(2)]
    s_sq = [[sem(f"s_sq{h}{b}") for b in range(2)] for h in range(2)]
    s_diff, s_gauss = sem("s_diff"), sem("s_gauss")
    s_pre, s_exp, s_cap, s_ln, s_ssp = sem("s_pre"), sem("s_exp"), sem("s_cap"), sem("s_ln"), sem("s_ssp")
    s_post, s_gate, s_prod, s_half, s_sum = sem("s_post"), sem("s_gate"), sem("s_prod"), sem("s_half"), sem("s_sum")

    def done(engine, s, tile, k, ahead):
        count = tile * SLOTS + (k + ahead)
        if isinstance(count, int) and count <= 0:
            return
        engine.wait_ge(s, count)

    def parts(k):
        return k // 4, (k // 2) % 2, k % 2

    def load_half(tile, h):
        done(SP, s_gauss, tile, 4 * h, -4)
        for b in range(2):
            row = adj_pairs[bass.ds(tile * 2 + b, 1), h * HALF:(h + 1) * HALF]
            SP.dma_start(E[h][b * NG:(b + 1) * NG, :], row.broadcast_to([NG, HALF])).then_inc(s_adj[h], 16)

    def load_squares(tile, h):
        for b in range(2):
            done(SP, s_gate, tile, 4 * h + 2 * b, -6)
            row = adj_sq[bass.ds(tile * 2 + b, 1), h * HALF:(h + 1) * HALF]
            SP.dma_start(A2[h][b][:], row.broadcast_to([P, HALF])).then_inc(s_sq[h][b], 16)

    for h in range(2):
        load_half(0, h)
        load_squares(0, h)
    with SP.Fori(1, TILES) as tile:
        for h in range(2):
            load_half(tile, h)
            load_squares(tile, h)

    def act_slot(tile, k):
        at = lagged(tile, k, 5)
        if at:
            t_, k_ = at
            done(A, s_cap, t_, k_, 1)
            A.activation(EX[k_ % 2][:], EX[k_ % 2][:], ACT.Ln, bias=half_col[:], scale=0.5).then_inc(s_ln, 1)
        at = lagged(tile, k, 4)
        if at:
            t_, k_ = at
            done(A, s_pre, t_, k_, 1)
            done(A, s_ssp, t_, k_, -1)
            A.activation(EX[k_ % 2][:], pre(k_ % 2), ACT.Exp, bias=cols["b1"][:]).then_inc(s_exp, 1)
        at = lagged(tile, k, 0)
        if at:
            h, r = k // 4, k % 4
            piece = slice(r * PIECE, (r + 1) * PIECE)
            if r == 0:
                A.wait_ge(s_adj[h], tile * 32 + 32)
                done(A, s_pre, tile, 4 * h, -4)
            A.activation(E[h][:, piece], E[h][:, piece], ACT.Square, bias=cols["off"][:]).then_inc(s_diff, 1)
            done(A, s_diff, tile, k, 1)
            A.activation(G[h][:, piece], E[h][:, piece], ACT.Exp, scale=COEFF).then_inc(s_gauss, 1)

    A.preload_act_table_set("natural_log_exp_and_others")
    pipeline(A, act_slot, 5)

    def pe_slot(tile, k):
        at = lagged(tile, k, 4)
        if at:
            t_, k_ = at
            h, b, c = parts(k_)
            done(PE, s_gauss, t_, 4 * h, 2 * c + 2)
            done(PE, s_ssp, t_, k_, -1)
            for n in range(2):
                last = PE.matmul(PS[:, 2 * (k_ % 2) + n, :], W1pad[:, b, :],
                                 G[h][:, c * CHUNK + n * BANK:c * CHUNK + (n + 1) * BANK], start=True, stop=True)
            last.then_inc(s_pre, 1)
        at = lagged(tile, k, 6)
        if at:
            t_, k_ = at
            done(PE, s_ssp, t_, k_, 1)
            done(PE, s_prod, t_, k_, -1)
            for n in range(2):
                last = PE.matmul(PS[:, 4 + 2 * (k_ % 2) + n, :], W2T[:],
                                 Hs[k_ % 2][:, n * BANK:(n + 1) * BANK], start=True, stop=True)
            last.then_inc(s_post, 1)

    pipeline(PE, pe_slot, 6)

    def i_major(ap):
        return ap.rearrange("p (i j) -> p i j", j=NODES)

    def gp_slot(tile, k):
        at = lagged(tile, k, 6)
        if at:
            t_, k_ = at
            h, b, c = parts(k_)
            GP.wait_ge(s_sq[h][b], t_ * 16 + 16)
            done(GP, s_prod, t_, k_, -1)
            GP.sem_inc(apart, 1)
            rf = rfT[:, bass.ds(t_ * P + b * NODES, NODES)].unsqueeze(1).broadcast_to([P, CHUNK // NODES, NODES])
            GP.tensor_tensor(i_major(GATE[k_ % 2][:]), rf, i_major(A2[h][b][:, c * CHUNK:(c + 1) * CHUNK]),
                             ALU.mult).then_inc(s_gate, 1)
        at = lagged(tile, k, 7)
        if at:
            t_, k_ = at
            done(GP, s_prod, t_, k_, 1)
            done(GP, s_sum, t_, k_, -1)
            product = i_major(PR[k_ % 2][:])
            GP.tensor_tensor(HP[k_ % 2][:].rearrange("p (i j) -> p i j", j=NODES // 2), product[:, :, 0:NODES // 2],
                             product[:, :, NODES // 2:], ALU.add).then_inc(s_half, 1)

    pipeline(GP, gp_slot, 7)

    def dve_slot(tile, k):
        at = lagged(tile, k, 5)
        if at:
            t_, k_ = at
            done(V, s_exp, t_, k_, 1)
            V.tensor_scalar(EX[k_ % 2][:], EX[k_ % 2][:], EXP_CAP, None, ALU.min).then_inc(s_cap, 1)
        at = lagged(tile, k, 7)
        if at:
            t_, k_ = at
            h, b, c = parts(k_)
            done(V, s_post, t_, k_, 1)
            done(V, s_gate, t_, k_, 1)
            done(V, s_half, t_, k_, -1)
            V.scalar_tensor_tensor(PR[k_ % 2][:], post(k_ % 2), cols["b2"][:], GATE[k_ % 2][:],
                                   ALU.add, ALU.mult).then_inc(s_prod, 1)
        at = lagged(tile, k, 5)
        if at:
            t_, k_ = at
            done(V, s_ln, t_, k_, 1)
            done(V, s_post, t_, k_, -1)
            V.scalar_tensor_tensor(Hs[k_ % 2][:], pre(k_ % 2), cols["b1l"][:], EX[k_ % 2][:],
                                   ALU.add, ALU.max).then_inc(s_ssp, 1)
        at = lagged(tile, k, 8)
        if at:
            t_, k_ = at
            h, b, c = parts(k_)
            done(V, s_half, t_, k_, 1)
            first = b * NODES + h * (NODES // 2) + c * (CHUNK // NODES)
            V.tensor_reduce(yT[:, bass.ds(t_ * P + first, CHUNK // NODES)],
                            HP[k_ % 2][:].rearrange("p (i j) -> p i j", j=NODES // 2), AX, ALU.add).then_inc(s_sum, 1)

    pipeline(V, dve_slot, 8)


DT = 8
DOT_GROUPS = TILES // DT


def attend_stage(nc, own, PS, apart, hw_d, hs_d, att_d, uv, w2sel, cols):
    V, A, PE, GP, SP = nc.vector, nc.scalar, nc.tensor, nc.gpsimd, nc.sync

    def sem(name):
        return own.enter_context(nc.semaphore(name))

    def sb(name, shape):
        return own.enter_context(nc.sbuf_tensor(name, shape, F32))

    Q = [sb(f"a_q{b}", [P, PAIRS]) for b in range(2)]
    QV, QU = sb("a_qv", [P, PAIRS]), sb("a_qu", [P, PAIRS])
    ST = [sb(f"a_w{b}", [P, P]) for b in range(2)]
    SI = [sb(f"a_silu{n}", [P, CHUNK]) for n in range(2)]
    W2 = [sb(f"a_w2{b}", [P, 2, 32]) for b in range(2)]
    ATT = sb("a_att", [P, BANK])
    VS, US = sb("a_vs", [P, NODES]), sb("a_us", [P, NODES])
    Z = 7
    att_out = att_d.rearrange("(g m q i) j -> g q m (i j)", g=DOT_GROUPS, q=4, i=BANK // NODES)

    s_w = [sem(f"s_w{b}") for b in range(2)]
    s_ones, s_v, s_u, s_q = sem("s_ones"), sem("s_v"), sem("s_u"), sem("s_q")
    s_vs, s_us = sem("s_vs"), sem("s_us")
    s_sel, s_first, s_silu, s_dot = sem("s_sel"), sem("s_first"), sem("s_silu"), sem("s_dot")
    s_tanh, s_out = sem("s_tanh"), sem("s_out")
    SILU_0, DOT_0, TANH_0, OUT_0, FIRST_0 = 2, 5, 1, 1, 5
    A.nop().then_inc(s_silu, SILU_0)
    PE.nop().then_inc(s_dot, DOT_0)
    PE.nop().then_inc(s_first, FIRST_0)
    A.nop().then_inc(s_tanh, TANH_0)
    SP.nop().then_inc(s_out, OUT_0)

    def rows_of(b):
        return slice(b * NODES, (b + 1) * NODES)

    def before(engine, s, count):
        if not isinstance(count, int) or count > 0:
            engine.wait_ge(s, count)

    def first_and_rest(engine, body):
        body(0)
        with engine.Fori(1, TILES) as tile:
            body(tile)

    def sp_tile(tile):
        for b in range(2):
            before(SP, s_first, (tile - 1) * 8 + (4 * b + 4 + FIRST_0))
            row = bass.ds(tile * P + b * NODES, NODES)
            SP.dma_start(ST[b][rows_of(b), :], hw_d[row, :]).then_inc(s_w[b], 16)
            SP.dma_start(ST[b][rows_of(1 - b), :], hs_d[row, :]).then_inc(s_w[b], 16)

    first_and_rest(SP, sp_tile)

    def by_pair(ap):
        return ap.rearrange("p (i j) -> p i j", j=NODES)

    square = [NODES, NODES, NODES]
    for b in range(2):
        GP.memset(Q[b][rows_of(1 - b), :], 1.0).then_inc(s_ones, 1)
    GP.wait_ge(s_ones, 2)
    for b in range(2):
        o = by_pair(Q[b][rows_of(1 - b), :])
        GP.affine_select(out=o, in_=o, compare_op=ALU.is_equal, fill=0.0, base=0,
                         pattern=[[-1, NODES], [0, NODES]], channel_multiplier=1).then_inc(s_ones, 1)

    def gp_tile(tile):
        for b in range(2):
            r = rows_of(b)
            before(GP, s_q, (tile - 1) * 2 + (b + 1))
            GP.wait_ge(s_vs, tile * 2 + (b + 1))
            GP.sem_inc(apart, 1)
            GP.affine_select(out=by_pair(QV[r, :]), in_=VS[r, :].unsqueeze(2).broadcast_to(square),
                             compare_op=ALU.is_equal, fill=0.0, base=0,
                             pattern=[[0, NODES], [-1, NODES]], channel_multiplier=1).then_inc(s_v, 1)
            GP.wait_ge(s_us, tile * 2 + (b + 1))
            GP.sem_inc(apart, 1)
            GP.affine_select(out=by_pair(QU[r, :]), in_=US[r, :].unsqueeze(1).broadcast_to(square),
                             compare_op=ALU.is_equal, fill=0.0, base=0,
                             pattern=[[-1, NODES], [0, NODES]], channel_multiplier=1).then_inc(s_u, 1)

    first_and_rest(GP, gp_tile)

    def copy_uv(tile, b):
        r = rows_of(b)
        V.tensor_copy(VS[r, :], uv[r, bass.ds((TILES + tile) * NODES, NODES)]).then_inc(s_vs, 1)
        V.tensor_copy(US[r, :], uv[r, bass.ds(tile * NODES, NODES)]).then_inc(s_us, 1)

    for b in range(2):
        copy_uv(0, b)
    with V.Fori(0, DOT_GROUPS) as g:
        with V.Fori(0, DT) as tl:
            for b in range(2):
                r = rows_of(b)
                graphs = g * (2 * DT) + tl * 2 + (b + 1)
                V.wait_ge(s_v, graphs)
                V.wait_ge(s_u, graphs)
                copy_uv(g * DT + (tl + 1), b)
                V.wait_ge(s_first, g * (8 * DT) + tl * 8 + (4 * b + 4 - 8 + FIRST_0))
                V.tensor_tensor(Q[b][r, :], QV[r, :], QU[r, :], ALU.add).then_inc(s_q, 1)
                V.wait_ge(s_dot, g * (8 * DT) + tl * 8 + (4 * b + 4 - 8 + DOT_0))
                V.sem_inc(apart, 1)
                for c in range(2):
                    last = V.tensor_copy(W2[b][:, c, :], w2sel[:, bass.ds(32 - 2 * b - c - tl * 4, 32)])
                last.then_inc(s_sel, 1)

    def pe_slot(g, tl, k):
        n = g * (8 * DT) + (tl * 8 + k)
        if not isinstance(tl, int) or tl < DT:
            b, c = k // 4, k % 4
            if c == 0:
                PE.wait_ge(s_q, g * (2 * DT) + (tl * 2 + (b + 1)))
                PE.wait_ge(s_w[b], g * (32 * DT) + (tl * 32 + 32))
            PE.wait_ge(s_silu, n + (-1 + SILU_0))
            for m in range(2):
                last = PE.matmul(PS[:, 2 * (k % 2) + m, :], ST[b][:],
                                 Q[b][:, c * CHUNK + m * BANK:c * CHUNK + (m + 1) * BANK], start=True, stop=True)
            last.then_inc(s_first, 1)
        if isinstance(tl, int) and tl == 0 and k == 0:
            return
        tl, k = (tl, k - 1) if k else (tl - 1, 7)
        b, c = k // 4, k % 4
        head = isinstance(tl, int) and tl == 0 and k < 2
        if head and k == 0:
            PE.wait_ge(s_tanh, g + TANH_0)
        if c == 0:
            PE.wait_ge(s_sel, g * (2 * DT) + (tl * 2 + (b + 1)))
        PE.wait_ge(s_silu, n + (0 + SILU_0))
        for m in range(2):
            q = (2 * c + m) % 4
            last = PE.matmul(PS[32 * q:32 * q + 32, Z, :], W2[b][:, (2 * c + m) // 4, :],
                             SI[k % 2][:, m * BANK:(m + 1) * BANK], start=head, stop=True, skip_group_check=True)
        last.then_inc(s_dot, 1)

    PE.wait_ge(s_ones, 4)
    with PE.Fori(0, DOT_GROUPS) as g:
        for k in range(8):
            pe_slot(g, 0, k)
        with PE.Fori(1, DT) as tl:
            for k in range(8):
                pe_slot(g, tl, k)
        pe_slot(g, DT, 0)

    with A.Fori(0, DOT_GROUPS) as g:
        with A.Fori(0, DT) as tl:
            for k in range(8):
                n = g * (8 * DT) + tl * 8 + k
                A.wait_ge(s_first, n + (1 + FIRST_0))
                A.wait_ge(s_dot, n + (-1 + DOT_0))
                pre = PS[:, 2 * (k % 2):2 * (k % 2) + 2, :].rearrange("p b n -> p (b n)")
                A.activation(SI[k % 2][:], pre, ACT.Silu, bias=cols["att_b1"][:]).then_inc(s_silu, 1)
        A.wait_ge(s_dot, g * (8 * DT) + (8 * DT + DOT_0))
        A.wait_ge(s_out, g * 64 + OUT_0)
        A.activation(ATT[:], PS[:, Z, :], ACT.Tanh, scale=0.5, bias=cols["att_b2"][:]).then_inc(s_tanh, 1)
        A.wait_ge(s_tanh, g + (1 + TANH_0))
        for q in range(4):
            A.dma_start(att_out[bass.ds(g, 1), q, :, :].rearrange("o m n -> (o m) n"),
                        ATT[32 * q:32 * q + 32, :]).then_inc(s_out, 16)
    SP.wait_ge(s_out, DOT_GROUPS * 64 + OUT_0)


def kernel(**inputs):
    import numpy as _np
    import concourse.bacc as _bacc
    from concourse import mybir as _mybir
    from concourse.bass_utils import run_bass_kernel_spmd as _run

    turned = {"adj": "adjT", "L0_gnn_W1": "W1T", "L0_gnn_W2": "W2T", "L0_gnn_Wa": "WaT", "L0_gnn_Wd1": "Wd1T",
              "L0_gnn_Wd2": "Wd2T", "L1_gnn_W": "WT", "L1_gnn_att_w1": "WattT", "L1_gnn_mlp_w1": "Wm1T",
              "L1_gnn_mlp_w2": "Wm2T"}
    straight = ["x", "adj", "L0_gnn_b1", "L0_gnn_b2", "L0_gnn_bd1", "L0_gnn_bd2", "L1_gnn_b_lin",
                "L1_gnn_att_b1", "L1_gnn_att_w2", "L1_gnn_att_b2", "L1_gnn_mlp_b1", "L1_gnn_mlp_b2",
                "L2_gnn_W", "L2_gnn_b", "L3_gnn_W_msg", "L3_gnn_W_upd"]
    arrays = {n: _np.ascontiguousarray(inputs[n]) for n in straight}
    for n, name in turned.items():
        arrays[name] = _np.ascontiguousarray(_np.swapaxes(_np.asarray(inputs[n]), -1, -2))
    nc = _bacc.Bacc("TRN2", target_bir_lowering=False, num_devices=1)
    t = {n: nc.dram_tensor("in_" + n, a.shape, _mybir.dt.from_np(a.dtype), kind="ExternalInput").ap()
         for n, a in arrays.items()}
    out = nc.dram_tensor("out_x", arrays["x"].shape, _mybir.dt.float32, kind="ExternalOutput").ap()
    build(nc, t, out)
    r = _run(nc, [{"in_" + n: a for n, a in arrays.items()}], core_ids=[0])
    return r.results[0]["out_x"]
```
